# Optimizing a Trainium2 kernel written in Bass

```python
import numpy as np
import jax
import jax.numpy as jnp

def _softmax(x, axis=-1):
    return jax.nn.softmax(x, axis=axis)

def _gelu(x):
    return jax.nn.gelu(x, approximate=True)

def _silu(x):
    return jax.nn.silu(x)

def _sigmoid(x):
    return jax.nn.sigmoid(x)

def _layernorm(x, axis=-1, eps=1e-05):
    m = jnp.mean(x, axis=axis, keepdims=True)
    v = jnp.var(x, axis=axis, keepdims=True)
    return (x - m) / jnp.sqrt(v + eps)

def _scatter_add(tgt, idx, src, axis=0):
    return tgt.at[idx].add(src)

def _segment_sum(src, seg, n):
    return jax.ops.segment_sum(src, seg, n)
kernel_name = 'mk_vit_tower_d2_tok_img768_r4_dcd939'

def setup_inputs(seed: int=0):
    np.random.seed(seed)
    _w = jnp.asarray

    def _rec_inputs():
        import jax
        import jax.numpy as jnp
        _rk = jax.random.key(seed)
        x = -0.00016672 + 0.999947 * jax.random.normal(jax.random.fold_in(_rk, 1), (8, 3, 128, 128), jnp.float32)
        return x
    x = _rec_inputs()

    def _L0_tok_setup():
        import jax, jax.numpy as jnp
        import numpy as np
        PH = PW = 16
        key = jax.random.key(seed)
        k1, k2, k3 = jax.random.split(key, 3)
        B, C, H, W_ = (64, 3, 96, 96)
        embed_dim = 192
        patch_dim = C * PH * PW
        x = jax.random.normal(k1, (B, C, H, W_), dtype=jnp.float32)
        W = jax.random.normal(k2, (embed_dim, patch_dim), dtype=jnp.float32) * 0.02
        b = jax.random.normal(k3, (embed_dim,), dtype=jnp.float32) * 0.02
        return {'x': x, 'W': W, 'b': b}
    _L0_tok_all = _L0_tok_setup()
    _L0_tok_in = {k: v for k, v in _L0_tok_all.items() if k in ('W', 'b')}
    del _L0_tok_all

    def _L0_attn_setup():
        import jax, jax.numpy as jnp
        import numpy as np
        HEADS = 12
        EPS = 1e-06

        def _rfm_softmax(seq, omega, query):
            d = seq.shape[-1]
            F = omega.shape[0]
            s = seq * float(d) ** (-0.25)
            s = jnp.einsum('bhld,fd->bhlf', s, omega)
            diag = jnp.sum(s, axis=-1, keepdims=True) / 2.0
            if query:
                m = jnp.max(s, axis=-1, keepdims=True)
            else:
                m = jnp.max(s, axis=(1, 3), keepdims=True)
            return float(F) ** (-0.5) * (jnp.exp(s - diag - m) + EPS)
        key = jax.random.key(seed)
        ks = jax.random.split(key, 5)
        B, L, E, F = (8, 128, 192, 64)
        Dh = E // HEADS
        x = jax.random.normal(ks[0], (B, L, E), dtype=jnp.float32)
        w_inp = jax.random.normal(ks[1], (1, E, 3 * E), dtype=jnp.float32) * 0.02
        b_inp = jnp.zeros((3 * E,), jnp.float32)
        w_out = jax.random.normal(ks[2], (1, E, E), dtype=jnp.float32) * 0.02
        b_out = jnp.zeros((E,), jnp.float32)
        g = jax.random.normal(ks[3], (Dh, F), dtype=jnp.float32)
        q, _ = jnp.linalg.qr(g)
        omega = q.T[:F].astype(jnp.float32)
        return {'x': x, 'w_inp': w_inp, 'b_inp': b_inp, 'w_out': w_out, 'b_out': b_out, 'omega': omega}
    _L0_attn_all = _L0_attn_setup()
    _L0_attn_in = {k: v for k, v in _L0_attn_all.items() if k in ('w_inp', 'b_inp', 'w_out', 'b_out', 'omega')}
    del _L0_attn_all

    def _L0_ffn_setup():
        import jax, jax.numpy as jnp
        import numpy as np
        G, E = (4, 8)
        KG, KE = (2, 2)
        D, M = (192, 768)
        SCALE = 0.02

        def _combine_weights(xf, Wg, bg, Wge, bge):
            N = xf.shape[0]
            glog = xf @ Wg + bg
            gtop, gidx = jax.lax.top_k(glog, KG)
            ggate = jax.nn.softmax(gtop, axis=-1)
            elog_all = jnp.einsum('nd,gde->nge', xf, Wge) + bge
            elog = jnp.take_along_axis(elog_all, gidx[:, :, None], axis=1)
            etop, eidx = jax.lax.top_k(elog, KE)
            egate = jax.nn.softmax(etop, axis=-1)
            w = ggate[:, :, None] * egate
            flat = gidx[:, :, None] * E + eidx
            comb = jnp.zeros((N, G * E), xf.dtype).at[jnp.arange(N)[:, None, None], flat].add(w)
            return comb
        key = jax.random.key(seed)
        ks = jax.random.split(key, 8)
        x = jax.random.normal(ks[0], (1, 128, D), jnp.float32)
        Wg = jax.random.normal(ks[1], (D, G), jnp.float32) * SCALE
        bg = jnp.zeros((G,), jnp.float32)
        Wge = jax.random.normal(ks[2], (G, D, E), jnp.float32) * SCALE
        bge = jnp.zeros((G, E), jnp.float32)
        W1 = jax.random.normal(ks[3], (G * E, D, M), jnp.float32) * SCALE
        b1 = jnp.zeros((G * E, M), jnp.float32)
        W2 = jax.random.normal(ks[4], (G * E, M, D), jnp.float32) * SCALE
        b2 = jnp.zeros((G * E, D), jnp.float32)
        return {'x': x, 'Wg': Wg, 'bg': bg, 'Wge': Wge, 'bge': bge, 'W1': W1, 'b1': b1, 'W2': W2, 'b2': b2}
    _L0_ffn_all = _L0_ffn_setup()
    _L0_ffn_in = {k: v for k, v in _L0_ffn_all.items() if k in ('Wg', 'bg', 'Wge', 'bge', 'W1', 'b1', 'W2', 'b2')}
    del _L0_ffn_all

    def _L1_attn_setup():
        import jax, jax.numpy as jnp
        import numpy as np
        ROPE_THETA = 10000.0

        def rope(x):
            B, S, D = x.shape
            half = D // 2
            inv_freq = 1.0 / ROPE_THETA ** (jnp.arange(half, dtype=jnp.float32) * 2.0 / D)
            ang = jnp.arange(S, dtype=jnp.float32)[:, None] * inv_freq[None, :]
            cos, sin = (jnp.cos(ang), jnp.sin(ang))
            x1, x2 = (x[..., 0::2], x[..., 1::2])
            r1 = x1 * cos - x2 * sin
            r2 = x1 * sin + x2 * cos
            return jnp.stack([r1, r2], axis=-1).reshape(B, S, D)
        key = jax.random.key(seed)
        ks = jax.random.split(key, 9)
        B, S, D = (4, 512, 192)
        w = 0.02
        return {'X': jax.random.normal(ks[0], (B, S, D), dtype=jnp.float32), 'Wq': jax.random.normal(ks[1], (D, D), dtype=jnp.float32) * w, 'bq': jnp.zeros((D,), dtype=jnp.float32), 'Wk': jax.random.normal(ks[2], (D, D), dtype=jnp.float32) * w, 'bk': jnp.zeros((D,), dtype=jnp.float32), 'Wv': jax.random.normal(ks[3], (D, D), dtype=jnp.float32) * w, 'bv': jnp.zeros((D,), dtype=jnp.float32), 'Wo': jax.random.normal(ks[4], (D, D), dtype=jnp.float32) * w, 'bo': jnp.zeros((D,), dtype=jnp.float32)}
    _L1_attn_all = _L1_attn_setup()
    _L1_attn_in = {k: v for k, v in _L1_attn_all.items() if k in ('Wq', 'bq', 'Wk', 'bk', 'Wv', 'bv', 'Wo', 'bo')}
    del _L1_attn_all

    def _L1_ffn_setup():
        import jax, jax.numpy as jnp
        import numpy as np
        from jax import lax
        DIM = 192
        INTER = 128
        E = 8
        G = 4
        TOPK_G = 2
        TOPK = 2
        ROUTE_SCALE = 1.0

        def _gate(x2, gate_weight, gate_bias):
            T = x2.shape[0]
            scores = jax.nn.sigmoid(x2 @ gate_weight.T)
            s = scores + gate_bias
            sv = s.reshape(T, G, E // G)
            top2, _ = lax.top_k(sv, 2)
            group_scores = top2.sum(-1)
            _, gidx = lax.top_k(group_scores, TOPK_G)
            gmask = jnp.zeros((T, G), bool).at[jnp.arange(T)[:, None], gidx].set(True)
            masked = jnp.where(gmask[:, :, None], sv, -jnp.inf).reshape(T, E)
            _, idx = lax.top_k(masked, TOPK)
            w = jnp.take_along_axis(scores, idx, axis=1)
            w = w / (w.sum(-1, keepdims=True) + 1e-06) * ROUTE_SCALE
            return (w, idx)
        key = jax.random.key(seed)
        ks = jax.random.split(key, 9)
        s = 1.0 / np.sqrt(DIM)
        si = 1.0 / np.sqrt(INTER)
        return {'x': jax.random.normal(ks[0], (4, 1024, DIM), jnp.float32), 'gate_weight': jax.random.uniform(ks[1], (E, DIM), jnp.float32, -s, s), 'gate_bias': jnp.zeros((E,), jnp.float32), 'w1': jax.random.uniform(ks[2], (E, INTER, DIM), jnp.float32, -s, s), 'w2': jax.random.uniform(ks[3], (E, DIM, INTER), jnp.float32, -si, si), 'w3': jax.random.uniform(ks[4], (E, INTER, DIM), jnp.float32, -s, s), 'sw1': jax.random.uniform(ks[5], (INTER, DIM), jnp.float32, -s, s), 'sw2': jax.random.uniform(ks[6], (DIM, INTER), jnp.float32, -si, si), 'sw3': jax.random.uniform(ks[7], (INTER, DIM), jnp.float32, -s, s)}
    _L1_ffn_all = _L1_ffn_setup()
    _L1_ffn_in = {k: v for k, v in _L1_ffn_all.items() if k in ('gate_weight', 'gate_bias', 'w1', 'w2', 'w3', 'sw1', 'sw2', 'sw3')}
    del _L1_ffn_all
    return {'x': x, 'L0_tok_W': _L0_tok_in['W'], 'L0_tok_b': _L0_tok_in['b'], 'L0_attn_w_inp': _L0_attn_in['w_inp'], 'L0_attn_b_inp': _L0_attn_in['b_inp'], 'L0_attn_w_out': _L0_attn_in['w_out'], 'L0_attn_b_out': _L0_attn_in['b_out'], 'L0_attn_omega': _L0_attn_in['omega'], 'L0_ffn_Wg': _L0_ffn_in['Wg'], 'L0_ffn_bg': _L0_ffn_in['bg'], 'L0_ffn_Wge': _L0_ffn_in['Wge'], 'L0_ffn_bge': _L0_ffn_in['bge'], 'L0_ffn_W1': _L0_ffn_in['W1'], 'L0_ffn_b1': _L0_ffn_in['b1'], 'L0_ffn_W2': _L0_ffn_in['W2'], 'L0_ffn_b2': _L0_ffn_in['b2'], 'L1_attn_Wq': _L1_attn_in['Wq'], 'L1_attn_bq': _L1_attn_in['bq'], 'L1_attn_Wk': _L1_attn_in['Wk'], 'L1_attn_bk': _L1_attn_in['bk'], 'L1_attn_Wv': _L1_attn_in['Wv'], 'L1_attn_bv': _L1_attn_in['bv'], 'L1_attn_Wo': _L1_attn_in['Wo'], 'L1_attn_bo': _L1_attn_in['bo'], 'L1_ffn_gate_weight': _L1_ffn_in['gate_weight'], 'L1_ffn_gate_bias': _L1_ffn_in['gate_bias'], 'L1_ffn_w1': _L1_ffn_in['w1'], 'L1_ffn_w2': _L1_ffn_in['w2'], 'L1_ffn_w3': _L1_ffn_in['w3'], 'L1_ffn_sw1': _L1_ffn_in['sw1'], 'L1_ffn_sw2': _L1_ffn_in['sw2'], 'L1_ffn_sw3': _L1_ffn_in['sw3']}

def reference(x, L0_tok_W, L0_tok_b, L0_attn_w_inp, L0_attn_b_inp, L0_attn_w_out, L0_attn_b_out, L0_attn_omega, L0_ffn_Wg, L0_ffn_bg, L0_ffn_Wge, L0_ffn_bge, L0_ffn_W1, L0_ffn_b1, L0_ffn_W2, L0_ffn_b2, L1_attn_Wq, L1_attn_bq, L1_attn_Wk, L1_attn_bk, L1_attn_Wv, L1_attn_bv, L1_attn_Wo, L1_attn_bo, L1_ffn_gate_weight, L1_ffn_gate_bias, L1_ffn_w1, L1_ffn_w2, L1_ffn_w3, L1_ffn_sw1, L1_ffn_sw2, L1_ffn_sw3):
    import jax
    import jax.numpy as jnp

    def _L0_tok_ref(x, W, b):
        import jax, jax.numpy as jnp
        import numpy as np
        PH = PW = 16
        B, C, H, Wd = x.shape
        Hp, Wp = (H // PH, Wd // PW)
        patches = x.reshape(B, C, Hp, PH, Wp, PW)
        patches = patches.transpose(0, 2, 4, 1, 3, 5).reshape(B, Hp * Wp, C * PH * PW)
        return jnp.einsum('bnp,ep->bne', patches, W) + b

    def _L0_attn_ref(x, w_inp, b_inp, w_out, b_out, omega):
        import jax, jax.numpy as jnp
        import numpy as np
        HEADS = 12
        EPS = 1e-06

        def _rfm_softmax(seq, omega, query):
            d = seq.shape[-1]
            F = omega.shape[0]
            s = seq * float(d) ** (-0.25)
            s = jnp.einsum('bhld,fd->bhlf', s, omega)
            diag = jnp.sum(s, axis=-1, keepdims=True) / 2.0
            if query:
                m = jnp.max(s, axis=-1, keepdims=True)
            else:
                m = jnp.max(s, axis=(1, 3), keepdims=True)
            return float(F) ** (-0.5) * (jnp.exp(s - diag - m) + EPS)
        B, L, E = x.shape
        H = HEADS
        Dh = E // H
        c = jnp.einsum('ble,eo->blo', x, w_inp[0]) + b_inp
        q, k, v = jnp.split(c, 3, axis=2)
        split = lambda t: t.reshape(B, L, H, Dh).transpose(0, 2, 1, 3)
        q, k, v = (split(q), split(k), split(v))
        qf = _rfm_softmax(q, omega, query=True)
        kf = _rfm_softmax(k, omega, query=False)
        qf = qf.transpose(2, 0, 1, 3)
        kf = kf.transpose(2, 0, 1, 3)
        vl = v.transpose(2, 0, 1, 3)
        rhs = jnp.cumsum(kf[..., None, :] * vl[..., :, None], axis=0)
        a = jnp.einsum('lbhdf,lbhf->lbhd', rhs, qf)
        denom = jnp.einsum('lbhf,lbhf->lbh', qf, jnp.cumsum(kf, axis=0))[..., None]
        a = a / (denom + EPS)
        a = a.transpose(1, 2, 0, 3)
        a = a.transpose(0, 2, 1, 3).reshape(B, L, E)
        out = jnp.einsum('ble,eo->blo', a, w_out[0]) + b_out
        return out

    def _L0_ffn_ref(x, Wg, bg, Wge, bge, W1, b1, W2, b2):
        import jax, jax.numpy as jnp
        import numpy as np
        G, E = (4, 8)
        KG, KE = (2, 2)
        D, M = (192, 768)
        SCALE = 0.02

        def _combine_weights(xf, Wg, bg, Wge, bge):
            N = xf.shape[0]
            glog = xf @ Wg + bg
            gtop, gidx = jax.lax.top_k(glog, KG)
            ggate = jax.nn.softmax(gtop, axis=-1)
            elog_all = jnp.einsum('nd,gde->nge', xf, Wge) + bge
            elog = jnp.take_along_axis(elog_all, gidx[:, :, None], axis=1)
            etop, eidx = jax.lax.top_k(elog, KE)
            egate = jax.nn.softmax(etop, axis=-1)
            w = ggate[:, :, None] * egate
            flat = gidx[:, :, None] * E + eidx
            comb = jnp.zeros((N, G * E), xf.dtype).at[jnp.arange(N)[:, None, None], flat].add(w)
            return comb
        shp = x.shape
        xf = x.reshape(-1, D)
        comb = _combine_weights(xf, Wg, bg, Wge, bge)
        h = jax.nn.gelu(jnp.einsum('nd,edm->nem', xf, W1) + b1, approximate=False)
        y = jnp.einsum('nem,emd->ned', h, W2) + b2
        out = jnp.einsum('ne,ned->nd', comb, y)
        return out.reshape(shp)

    def _L1_attn_ref(X, Wq, bq, Wk, bk, Wv, bv, Wo, bo):
        import jax, jax.numpy as jnp
        import numpy as np
        ROPE_THETA = 10000.0

        def rope(x):
            B, S, D = x.shape
            half = D // 2
            inv_freq = 1.0 / ROPE_THETA ** (jnp.arange(half, dtype=jnp.float32) * 2.0 / D)
            ang = jnp.arange(S, dtype=jnp.float32)[:, None] * inv_freq[None, :]
            cos, sin = (jnp.cos(ang), jnp.sin(ang))
            x1, x2 = (x[..., 0::2], x[..., 1::2])
            r1 = x1 * cos - x2 * sin
            r2 = x1 * sin + x2 * cos
            return jnp.stack([r1, r2], axis=-1).reshape(B, S, D)
        NUM_HEADS = 12
        B, S, D = X.shape
        hd = D // NUM_HEADS
        q = rope(X @ Wq + bq)
        k = rope(X @ Wk + bk)
        v = X @ Wv + bv
        qh = q.reshape(B, S, NUM_HEADS, hd)
        kh = k.reshape(B, S, NUM_HEADS, hd)
        vh = v.reshape(B, S, NUM_HEADS, hd)
        scores = jnp.einsum('bqhd,bkhd->bhqk', qh, kh) / jnp.sqrt(jnp.float32(hd))
        causal = jnp.tril(jnp.ones((S, S), dtype=bool))
        scores = jnp.where(causal[None, None, :, :], scores, -jnp.inf)
        weights = jax.nn.softmax(scores, axis=-1)
        out = jnp.einsum('bhqk,bkhd->bqhd', weights, vh).reshape(B, S, D)
        return out @ Wo + bo

    def _L1_ffn_ref(x, gate_weight, gate_bias, w1, w2, w3, sw1, sw2, sw3):
        import jax, jax.numpy as jnp
        import numpy as np
        from jax import lax
        DIM = 192
        INTER = 128
        E = 8
        G = 4
        TOPK_G = 2
        TOPK = 2
        ROUTE_SCALE = 1.0

        def _gate(x2, gate_weight, gate_bias):
            T = x2.shape[0]
            scores = jax.nn.sigmoid(x2 @ gate_weight.T)
            s = scores + gate_bias
            sv = s.reshape(T, G, E // G)
            top2, _ = lax.top_k(sv, 2)
            group_scores = top2.sum(-1)
            _, gidx = lax.top_k(group_scores, TOPK_G)
            gmask = jnp.zeros((T, G), bool).at[jnp.arange(T)[:, None], gidx].set(True)
            masked = jnp.where(gmask[:, :, None], sv, -jnp.inf).reshape(T, E)
            _, idx = lax.top_k(masked, TOPK)
            w = jnp.take_along_axis(scores, idx, axis=1)
            w = w / (w.sum(-1, keepdims=True) + 1e-06) * ROUTE_SCALE
            return (w, idx)
        B, S, D = x.shape
        x2 = x.reshape(-1, D)
        T = x2.shape[0]
        weights, indices = _gate(x2, gate_weight, gate_bias)
        cw = jnp.zeros((T, E), x.dtype).at[jnp.arange(T)[:, None], indices].add(weights)
        h1 = jnp.einsum('td,eid->tei', x2, w1)
        h3 = jnp.einsum('td,eid->tei', x2, w3)
        h = jax.nn.silu(h1) * h3
        y = jnp.einsum('tei,edi,te->td', h, w2, cw)
        z = jax.nn.silu(x2 @ sw1.T) * (x2 @ sw3.T) @ sw2.T
        return (y + z).reshape(B, S, D)
    h = _L0_tok_ref(x, L0_tok_W, L0_tok_b)
    h = h + _L0_attn_ref(_layernorm(h, axis=-1), L0_attn_w_inp, L0_attn_b_inp, L0_attn_w_out, L0_attn_b_out, L0_attn_omega)
    h = h + _L0_ffn_ref(_layernorm(h, axis=-1), L0_ffn_Wg, L0_ffn_bg, L0_ffn_Wge, L0_ffn_bge, L0_ffn_W1, L0_ffn_b1, L0_ffn_W2, L0_ffn_b2)
    h = h + _L1_attn_ref(_layernorm(h, axis=-1), L1_attn_Wq, L1_attn_bq, L1_attn_Wk, L1_attn_bk, L1_attn_Wv, L1_attn_bv, L1_attn_Wo, L1_attn_bo)
    h = h + _L1_ffn_ref(_layernorm(h, axis=-1), L1_ffn_gate_weight, L1_ffn_gate_bias, L1_ffn_w1, L1_ffn_w2, L1_ffn_w3, L1_ffn_sw1, L1_ffn_sw2, L1_ffn_sw3)
    return h

_drawn_inputs = setup_inputs


def setup_inputs(seed=0):
    import zlib

    import numpy as np

    out = dict(_drawn_inputs(seed))
    spreads = {'L0_attn_b_inp': (0.0, 0.1),
     'L0_attn_b_out': (0.0, 0.1),
     'L0_ffn_bg': (0.0, 0.301),
     'L0_ffn_bge': (0.0, 0.1),
     'L0_ffn_b1': (0.0, 0.1),
     'L0_ffn_b2': (0.0, 0.1),
     'L1_attn_bq': (0.0, 0.8),
     'L1_attn_bk': (0.0, 0.8),
     'L1_attn_bv': (0.0, 0.1),
     'L1_attn_bo': (0.0, 0.1),
     'L1_ffn_gate_bias': (0.0, 0.1)}
    factors = {'L0_attn_omega': 3.451, 'L1_attn_Wq': 8.0, 'L1_attn_Wk': 8.0}
    for name, (base, spread) in spreads.items():
        noise = np.random.default_rng([zlib.crc32(name.encode()), seed]).standard_normal(out[name].shape)
        drawn = base * np.exp(spread * noise) if base else spread * noise
        out[name] = jnp.asarray(drawn.astype(out[name].dtype))
    for name, factor in factors.items():
        out[name] = (out[name] * factor).astype(out[name].dtype)
    return out
```

```python
from contextlib import ExitStack

import numpy as np

import concourse.bass as bass
from concourse import mybir

F32 = mybir.dt.float32
I32 = mybir.dt.int32
U32 = mybir.dt.uint32
ALU = mybir.AluOpType
ACT = mybir.ActivationFunctionType
X = mybir.AxisListType.X

P = 128
NIMG, NCH, IMG, PATCH = 8, 3, 128, 16
SIDE = IMG // PATCH
SEQ = SIDE * SIDE
TOK = NIMG * SEQ
NT = TOK // P
IPT = P // SEQ
D = 192
DA, DB = P, D - P
PD = NCH * PATCH * PATCH
KP = PD // P
H, HD = 12, 16
HPAD = 32
HG = P // HPAD
HB = H // HG
NPAIR = H // 2
VW = HD + 1
LN_EPS = 1e-5
RFM_EPS = 1e-6
G, EG = 4, 8
NE = G * EG
HID = 768
KH = HID // P
PICKS = 4
NOV = (TOK * PICKS) // P - 1
SLOTS = (NE + NOV) * P
XW = D + DB
RING = 4
E1, INTER = 8, 128
N1 = E1 + 1
BIG = 1.0e30

BANK = 512

CONST = {}
_at = 0
for _name, _w in (("ident", P), ("causal", SEQ), ("future", SEQ), ("rope_cos", D), ("rope_sin", D),
                  ("before", P), ("headblock", P // HD), ("tie4", 16), ("tie8", 64),
                  ("first_slot", NE), ("ones", P), ("index", NE), ("row", 1), ("ln_eps", 1)):
    CONST[_name] = (_at, _at + _w)
    _at += _w
NCONST = _at


def shape_constants():
    c = np.zeros((P, NCONST), np.float32)

    def put(name, a):
        c[:, CONST[name][0]:CONST[name][1]] = a

    row = np.arange(P)
    pos = row % SEQ
    put("ident", np.eye(P))
    put("causal", np.arange(SEQ)[None, :] <= pos[:, None])
    put("future", -BIG * (np.arange(SEQ)[None, :] > pos[:, None]))
    half = D // 2
    freq = (1.0 / (np.float32(10000.0) ** (np.arange(half, dtype=np.float32) * np.float32(2.0) / np.float32(D)))).astype(np.float32)
    ang = pos.astype(np.float32)[:, None] * freq[None, :]
    put("rope_cos", np.repeat(np.cos(ang), 2, axis=1))
    put("rope_sin", np.stack([-np.sin(ang), np.sin(ang)], axis=2).reshape(P, D))
    put("before", row[:, None] < row[None, :])
    put("headblock", (row[:, None] // HD == np.arange(P // HD)[None, :]) * float(HD) ** -0.25)
    for name, n in (("tie4", G), ("tie8", EG)):
        put(name, (np.arange(n)[None, :] < np.arange(n)[:, None]).reshape(1, n * n))
    put("first_slot", np.arange(NE)[None, :] * P)
    put("ones", 1.0)
    put("index", np.arange(NE)[None, :])
    put("row", row[:, None])
    put("ln_eps", LN_EPS)
    return c


def vit_tower(nc, dram, consts, out, dbg=None):
    es = ExitStack()
    with es:
        def sb(name, shape, dt=F32):
            return es.enter_context(nc.sbuf_tensor(name, shape, dt))

        def sem(name):
            return es.enter_context(nc.semaphore(name))

        x_slots = nc.dram_tensor("x_slots", (SLOTS, XW), F32).ap()
        y_slots = nc.dram_tensor("y_slots", (SLOTS, D), F32).ap()

        cst = sb("cst", [P, NCONST])

        def const(name, rows=P, cols=None):
            a, b = CONST[name]
            return cst[0:rows, a:(b if cols is None else a + cols)]

        early = sb("early", [P, 2 * KP * TOK])
        x_in = early[:, 0:KP * TOK].rearrange("p (c n) -> p c n", c=NCH)
        patchesT = early[:, KP * TOK:2 * KP * TOK].rearrange("p (k n) -> p k n", k=KP)
        w13_raw = early[:, 0:2 * N1 * P].rearrange("p (e m d) -> p e m d", e=N1, m=2)
        w13_raw_tail = early[:, 2 * N1 * P:3 * N1 * P].rearrange("p (e c) -> p e c", e=N1)
        w2_raw = early[:, 3 * N1 * P:4 * N1 * P].rearrange("p (e c) -> p e c", e=N1)
        w2_raw_tail = early[0:DB, 4 * N1 * P:5 * N1 * P].rearrange("p (e c) -> p e c", e=N1)

        wtok = sb("wtok", [P, 2, PD])
        wtokT = sb("wtokT", [P, KP, D])
        btok = sb("btok", [P, D])
        h = sb("h", [P, NT, D])
        hb = sb("hb", [P, NT, D])
        stats = sb("stats", [P, NT, 6])
        mv = sb("mv", [P, NT, 2])
        rstd = sb("rstd", [P, NT, 1])
        xn = sb("xn", [P, NT, XW])
        xnT = sb("xnT", [P, 2, TOK])

        wqkv0 = sb("wqkv0", [P, 2, 3 * D])
        bqk0 = sb("bqk0", [P, 3])
        bv = [sb(f"bv{a}", [P, D // 2]) for a in range(2)]
        wo = [sb(f"wo{a}", [P, 2, D]) for a in range(2)]
        bo = [sb(f"bo{a}", [P, D]) for a in range(2)]
        omega8 = sb("omega8", [HD, P // HD, HD])
        omega_bd = sb("omega_bd", [P, P])
        wqkv1 = sb("wqkv1", [P, 2, 3 * D])
        bqk1 = sb("bqk1", [P, 2 * D])

        qkT0 = sb("qkT0", [P, 3, TOK])
        qk_pad = sb("qk_pad", [P, NT, 2 * H, HPAD])
        qk_padT = sb("qk_padT", [P, NT, 2 * HB, P])
        fsum = sb("fsum", [P, NT, 2 * H])
        foff = sb("foff", [P, NT, 2 * H])
        fmax = sb("fmax", [P, NT, 1])
        fexp = sb("fexp", [P, NT, 2 * H, HD])
        turned = sb("turned", [P, NT, 2 * D])
        probs = sb("probs", [P, NT, H, SEQ])
        probsT = sb("probsT", [P, NT, NPAIR, P])
        x_by_col = probsT[:, :, :, :].rearrange("p t j n -> p (t j n)").rearrange("p (c w n) -> p c w n", c=NCH, w=SIDE)
        rowmax = sb("rowmax", [P, NT, H])
        v_bd = sb("v_bd", [P, NIMG, NPAIR, 2 * VW])
        rden = sb("rden", [P, NT, H])
        att = sb("att", [P, NT, XW])
        attT = sb("attT", [P, NT, 2, P])

        wroute = sb("wroute", [P, 2, G + NE])
        broute = sb("broute", [P, G + NE])
        b1_rows, b2_rows = sb("b1_rows", [NE, HID]), sb("b2_rows", [NE, D])
        b1T = sb("b1T", [P, KH, NE])
        b1T_ov = sb("b1T_ov", [P, KH, NOV])
        ggl, gel = sb("ggl", [P, NT, G]), sb("gel", [P, NT * G, EG])
        rank_g, rank_e = sb("rank_g", [P, NT, G]), sb("rank_e", [P, NT * G, EG])
        sel_g, sel_e = sb("sel_g", [P, NT, G]), sb("sel_e", [P, NT * G, EG])
        chosen = sb("chosen", [P, NT, NE])
        gate_in = sb("gate_in", [P, NT * (G + NE)])
        gate_g, gate_e = gate_in[:, 0:NT * G], gate_in[:, NT * G:NT * (G + NE)]
        top = sb("top", [P, NT * (1 + G)])
        comb = sb("comb", [P, NT, NE])
        combT = sb("combT", [NE, TOK])
        extra = sb("extra", [P, NE])
        extra_sum = sb("extra_sum", [P, NE])
        shift = sb("shift", [P, NE])
        slot = sb("slot", [P, NT, NE])
        extra_col, extra_at, extra_end = sb("extra_col", [NE, 1]), sb("extra_at", [NE, 1]), sb("extra_end", [NE, 1])
        ov_from, ov_onehot = sb("ov_from", [NE, NOV]), sb("ov_onehot", [NE, NOV])
        ov_info = sb("ov_info", [1, NOV + 1], I32)
        pick_g, pick_e = sb("pick_g", [P, 2, NT, G]), sb("pick_e", [P, 2, NT, NE])
        pick = sb("pick", [P, PICKS, NT, NE])
        picked = sb("picked", [P, PICKS * NT, NE])
        pick_slot, pick_w = sb("pick_slot", [P, PICKS * NT]), sb("pick_w", [P, PICKS * NT])
        pick_slot_u = sb("pick_slot_u", [P, PICKS * NT], U32)
        beats = fexp[:, :, :, :].rearrange("p t h f -> p (t h f)")[:, 0:NT * G * EG * EG]
        ties = turned[:, :, :].rearrange("p t n -> p (t n)")[:, 0:NT * G * EG * EG]
        zeros = sb("zeros", [P, XW])
        w1 = sb("w1", [P, RING, HID])
        w1_tail = sb("w1_tail", [P, RING, HID // 2])
        w2 = sb("w2", [P, RING, KH, D])
        x_rows = qkT0[:, :, :].rearrange("p c n -> p (c n)")[:, 0:RING * XW].rearrange("p (u n) -> p u n", u=RING)
        after_exp = fexp[:, :, :, :].rearrange("p t h f -> p (t h f)")
        x_rowsT = after_exp[:, 0:4 * P].rearrange("p (b c n) -> p b c n", b=2, c=2)
        y_rows = after_exp[:, 4 * P:4 * P + RING * D].rearrange("p (u n) -> p u n", u=RING)
        hidden = turned[:, :, :].rearrange("p t n -> p (t n)").rearrange("p (b c n) -> p b c n", b=2, c=KH)
        y_back = qk_padT[:, :, :, :].rearrange("p t j n -> p t (j n)").rearrange("p t (k d) -> p t k d", k=PICKS)

        w13T = w1[:, :, :].rearrange("p u n -> p (u n)")[:, 0:2 * N1 * P].rearrange("p (e m i) -> p e m i", e=N1, m=2)
        w13T_tail = w1_tail[:, :, :].rearrange("p u n -> p (u n)")[:, 0:N1 * P].rearrange("p (e i) -> p e i", e=N1)
        w2T = w2[:, :, :, :].rearrange("p u c d -> p (u c d)")[:, 0:N1 * D].rearrange("p (e d) -> p e d", e=N1)
        gate_rows, gate_wT, gate_b = sb("gate_rows", [E1, XW]), sb("gate_wT", [P, 2, E1]), sb("gate_b", [P, E1])
        score, biased = sb("score", [P, NT, E1]), sb("biased", [P, NT, E1])
        group_sum, shut = sb("group_sum", [P, NT, G]), sb("shut", [P, NT, G])
        rank_1 = sb("rank_1", [P, NT, E1])
        score_sum, cw = sb("score_sum", [P, NT]), sb("cw", [P, NT, E1])
        after_probs = probs[:, :, :, :].rearrange("p t h k -> p (t h k)")
        rope_swap = after_probs.rearrange("p (t n) -> p t n", t=NT)
        silu = after_probs[:, 0:2 * TOK].rearrange("p (b n) -> p b n", b=2)
        gated = after_probs[:, 2 * TOK:4 * TOK].rearrange("p (b n) -> p b n", b=2)

        ps = es.enter_context(nc.psum_tensor("ps", [P, 8, BANK], F32))

        x_in_dma = [sem(f"x_in_dma{c}") for c in range(NCH)]
        wtok_dma, const_dma, attn0_dma, attn1_dma = sem("wtok_dma"), sem("const_dma"), sem("attn0_dma"), sem("attn1_dma")
        pads_zeroed = sem("pads_zeroed")
        x_by_col_ready = [sem(f"x_by_col_ready{c}") for c in range(NCH)]
        wtokT_mm, wtokT_sb = sem("wtokT_mm"), sem("wtokT_sb")
        patches_mm, patches_act, patches_dve = sem("patches_mm"), sem("patches_act"), sem("patches_dve")
        embed_mm = sem("embed_mm")
        h_ready, hb_ready = sem("h_ready"), sem("hb_ready")
        moments, deviation = sem("moments"), sem("deviation")
        xn_ready, xnT_mm, xnT_sb = sem("xn_ready"), sem("xnT_mm"), sem("xnT_sb")
        omega_mm, omega_sb = sem("omega_mm"), sem("omega_sb")
        qkT0_mm, qkT0_sb = sem("qkT0_mm"), sem("qkT0_sb")
        v_mm, v_sb = sem("v_mm"), sem("v_sb")
        qk_mm, feat_centred, feat_exp, qk_pad_ready = sem("qk_mm"), sem("feat_centred"), sem("feat_exp"), sem("qk_pad_ready")
        rope_sum = sem("rope_sum")
        qk_padT_mm, qk_padT_sb = sem("qk_padT_mm"), sem("qk_padT_sb")
        scores_mm, scores_read, centred, probs_exp = sem("scores_mm"), sem("scores_read"), sem("centred"), sem("probs_exp")
        probsT_mm, probsT_sb = sem("probsT_mm"), sem("probsT_sb")
        att_mm, att_ready, attT_mm, attT_sb, proj_mm = sem("att_mm"), sem("att_ready"), sem("attT_mm"), sem("attT_sb"), sem("proj_mm")
        route_dma, zeros_dma, zeros_ready = sem("route_dma"), sem("zeros_dma"), sem("zeros_ready")
        logits_mm, chosen_ready, counts_mm = sem("logits_mm"), sem("chosen_ready"), sem("counts_mm")
        gates_centred, gates_exp, comb_ready = sem("gates_centred"), sem("gates_exp"), sem("comb_ready")
        extra_col_ready, extra_at_mm, ov_onehot_ready, ov_mm, ov_info_ready = (
            sem("extra_col_ready"), sem("extra_at_mm"), sem("ov_onehot_ready"), sem("ov_mm"), sem("ov_info_ready"))
        b1T_sb, slots_ready, scatter_dma = sem("b1T_sb"), sem("slots_ready"), sem("scatter_dma")
        combT_mm, combT_sb, b2_mm, b2_added = sem("combT_mm"), sem("combT_sb"), sem("b2_mm"), sem("b2_added")
        w_dma, x_dma, y_dma = ([sem(f"{n}{u}") for u in range(RING)] for n in ("w_dma", "x_dma", "y_dma"))
        rowsT_mm, rowsT_sb, up_mm, gelu_done, down_mm, y_ready = (
            sem("rowsT_mm"), sem("rowsT_sb"), sem("up_mm"), sem("gelu_done"), sem("down_mm"), sem("y_ready"))
        ov_stored = sem("ov_stored")
        ov_w_dma, ov_x_dma, ov_y_dma = sem("ov_w_dma"), sem("ov_x_dma"), sem("ov_y_dma")
        ov_rowsT_mm, ov_rowsT_sb, ov_up_mm, ov_gelu, ov_down_mm, ov_y_ready = (
            sem("ov_rowsT_mm"), sem("ov_rowsT_sb"), sem("ov_up_mm"), sem("ov_gelu"), sem("ov_down_mm"), sem("ov_y_ready"))
        y_stored, y_back_dma = sem("y_stored"), [sem(f"y_back_dma{t}") for t in range(NT)]
        ffn_dma, ffn_wT_mm, ffn_wT_sb = sem("ffn_dma"), sem("ffn_wT_mm"), sem("ffn_wT_sb")
        qk_biased, rope_cos_part = sem("qk_biased"), sem("rope_cos_part")
        gate_mm, score_ready = sem("gate_mm"), sem("score_ready")
        up1_mm, silu_done, gated_ready, down1_mm, summed = sem("up1_mm"), sem("silu_done"), sem("gated_ready"), sem("down1_mm"), sem("summed")
        dve_step = sem("dve_step")
        out_dma = sem("out_dma")

        ident = const("ident")
        NATTN = 8

        def load_columns(q, dst, src, done):
            q.dma_start(dst[:, 0, :], src[0:DA, :]).then_inc(done, 16)
            q.dma_start(dst[0:DB, 1, :], src[DA:D, :]).then_inc(done, 16)

        def load_bv(q, dst, src, done):
            s = src.rearrange("(j p d) -> p j d", p=2, d=HD)
            for par in range(2):
                q.dma_start(dst[par * SEQ:(par + 1) * SEQ, :].rearrange("p (j d) -> p j d", d=HD),
                            s[par:par + 1].to_broadcast([SEQ, NPAIR, HD])).then_inc(done, 16)

        def load_row(q, dst, src, done):
            q.dma_start(dst[:, :], src.unsqueeze(0).to_broadcast([P, src.shape[0]])).then_inc(done, 16)

        def patch_job(copy, n):
            c, part = n // 2, n % 2
            dst = patchesT[:, 2 * c:2 * c + 2, :].rearrange("p k (s w) -> p k s w", w=SIDE)[:, :, :, part * 4:part * 4 + 4]
            src = ps[:, PATCH_BANK[n], :].rearrange("p (w k s) -> p k s w", w=4, k=2)
            return copy(dst, src)

        def regroup_channel(copy, c):
            return copy(x_by_col[:, c].rearrange("p w (r q) -> p w r q", q=PATCH),
                        x_in[:, c, :].rearrange("p (r w q) -> p w r q", w=SIDE, q=PATCH))

        block = es.enter_context(nc.Block())

        @block.sync
        def _(sp):
            xv = dram["x"].rearrange("b c (hp hh r) w -> c hh b hp (r w)", hp=SIDE, hh=2)
            for c in range(NCH):
                for hh in range(2):
                    sp.dma_start(x_in[hh * SEQ:(hh + 1) * SEQ, c, :], xv[c, hh]).then_inc(x_in_dma[c], 16)
            w1v = wqkv1[:, :, :]
            for n, name in enumerate(("L1_attn_Wq", "L1_attn_Wk", "L1_attn_Wv")):
                load_columns(sp, w1v[:, :, n * D:(n + 1) * D], dram[name], attn1_dma)
            load_row(sp, bqk1[:, 0:D], dram["L1_attn_bq"], attn1_dma)
            load_row(sp, bqk1[:, D:2 * D], dram["L1_attn_bk"], attn1_dma)
            load_bv(sp, bv[1], dram["L1_attn_bv"], attn1_dma)
            load_columns(sp, wo[1], dram["L1_attn_Wo"], attn1_dma)
            load_row(sp, bo[1], dram["L1_attn_bo"], attn1_dma)

            pw = dram["L0_ffn_Wge"].rearrange("g d e -> d g e")
            for c, (a, b) in enumerate(((0, DA), (DA, D))):
                sp.dma_start(wroute[0:b - a, c, 0:G], dram["L0_ffn_Wg"][a:b, :]).then_inc(route_dma, 16)
                sp.dma_start(wroute[0:b - a, c, G:G + NE].rearrange("p (g e) -> p g e", g=G), pw[a:b]).then_inc(route_dma, 16)
            sp.dma_start(broute[:, 0:G], dram["L0_ffn_bg"].unsqueeze(0).to_broadcast([P, G])).then_inc(route_dma, 16)
            sp.dma_start(broute[:, G:G + NE], dram["L0_ffn_bge"].rearrange("g e -> (g e)").unsqueeze(0).to_broadcast([P, NE])).then_inc(route_dma, 16)
            sp.dma_start(b1_rows[:, :], dram["L0_ffn_b1"]).then_inc(route_dma, 16)
            sp.dma_start(b2_rows[:, :], dram["L0_ffn_b2"]).then_inc(route_dma, 16)
            sp.wait_ge(zeros_ready, 1)
            sp.dma_start(x_slots.rearrange("(r p) c -> p r c", p=P), zeros[:, :].unsqueeze(1).to_broadcast([P, SLOTS // P, XW])).then_inc(zeros_dma, 16)

            sp.dma_start(y_slots[NE * P:SLOTS, :].rearrange("(r p) c -> p r c", p=P), zeros[:, 0:D].unsqueeze(1).to_broadcast([P, NOV, D])).then_inc(zeros_dma, 16)

            def load_expert(e, u, done):
                one = bass.ds(e, 1)
                w1d = dram["L0_ffn_W1"][one, :, :].rearrange("a d m -> (a d) m")
                sp.dma_start(w1[:, u, :], w1d[0:DA, :]).then_inc(done, 16)
                sp.dma_start(w1_tail[0:DB, u, :], w1d[DA:D, 0:HID // 2]).then_inc(done, 16)
                sp.dma_start(w1_tail[DB:P, u, :], w1d[DA:D, HID // 2:HID]).then_inc(done, 16)
                sp.dma_start(w2[:, u], dram["L0_ffn_W2"][one, :, :].rearrange("a (c p) d -> p (a c) d", p=P)).then_inc(done, 16)

            def load_rows(tile, u, done):
                sp.dma_start(x_rows[:, u, :], x_slots[bass.ds(tile * P, P), :]).then_inc(done, 16)

            for u in range(RING):
                load_expert(u, u, w_dma[u])
            sp.wait_ge(embed_mm, NT)
            for m, (name, shared) in enumerate((("L1_ffn_w1", "L1_ffn_sw1"), ("L1_ffn_w3", "L1_ffn_sw3"))):
                tail = slice(m * DB, (m + 1) * DB)
                sp.dma_start(w13_raw[:, 0, m, :], dram[shared][:, 0:DA]).then_inc(ffn_dma, 16)
                sp.dma_start(w13_raw_tail[:, 0, tail], dram[shared][:, DA:D]).then_inc(ffn_dma, 16)
                w = dram[name].rearrange("e i d -> i e d")
                sp.dma_start(w13_raw[:, 1:N1, m, :], w[:, :, 0:DA]).then_inc(ffn_dma, 16)
                sp.dma_start(w13_raw_tail[:, 1:N1, tail], w[:, :, DA:D]).then_inc(ffn_dma, 16)
            sp.dma_start(w2_raw[:, 0, :], dram["L1_ffn_sw2"][0:DA, :]).then_inc(ffn_dma, 16)
            sp.dma_start(w2_raw_tail[:, 0, :], dram["L1_ffn_sw2"][DA:D, :]).then_inc(ffn_dma, 16)
            w = dram["L1_ffn_w2"].rearrange("e d i -> d e i")
            sp.dma_start(w2_raw[:, 1:N1, :], w[0:DA]).then_inc(ffn_dma, 16)
            sp.dma_start(w2_raw_tail[:, 1:N1, :], w[DA:D]).then_inc(ffn_dma, 16)
            sp.dma_start(gate_rows[:, 0:D], dram["L1_ffn_gate_weight"]).then_inc(ffn_dma, 16)
            sp.dma_start(gate_rows[:, D:XW], dram["L1_ffn_gate_weight"][:, DA:D]).then_inc(ffn_dma, 16)
            load_row(sp, gate_b, dram["L1_ffn_gate_bias"], ffn_dma)
            sp.wait_ge(scatter_dma, 16 * PICKS * NT)
            for u in range(RING):
                load_rows(u, u, x_dma[u])

            def feed(i, more):
                for u in range(RING):
                    if more:
                        sp.wait_ge(down_mm, i * RING + u + 1)
                        load_expert((i + 1) * RING + u, u, w_dma[u])
                        load_rows((i + 1) * RING + u, u, x_dma[u])
                    sp.wait_ge(y_ready, i * RING + u + 1)
                    sp.dma_start(y_slots[bass.ds((i * RING + u) * P, P), :], y_rows[:, u, :]).then_inc(y_dma[u], 16)

            with sp.Fori(0, ROUNDS - 1) as i:
                feed(i, True)
            feed(ROUNDS - 1, False)
            sp.wait_ge(ov_info_ready, 2)
            tiles = sp.value_load(ov_info[0:1, NOV:NOV + 1], min_val=0, max_val=NOV)
            for u in range(RING):
                sp.wait_ge(y_dma[u], 16 * ROUNDS)
            with sp.Fori(0, NOV) as i:
                with sp.If(tiles > i):
                    e = sp.value_load(ov_info[0:1, bass.ds(i, 1)], min_val=0, max_val=NE - 1)
                    load_expert(e, 0, ov_w_dma)
                    load_rows(i + NE, 0, ov_x_dma)
                    sp.wait_ge(ov_y_ready, i + 1)
                    sp.dma_start(y_slots[bass.ds((i + NE) * P, P), :], y_rows[:, 0, :]).then_inc(ov_y_dma, 16)
                    sp.wait_ge(ov_y_dma, 16 * (i + 1))
                    sp.sem_inc(ov_stored, 1)
                sp.nop()
            sp.sem_inc(y_stored, 1)

            sp.wait_ge(summed, N1)
            sp.dma_start(out.rearrange("(t i) s d -> (i s) t d", t=NT), h[:, :, :]).then_inc(out_dma, 16)
            sp.wait_ge(out_dma, 16)

        @block.gpsimd
        def _(pool):
            pool.memset(zeros[:, :], 0.0).then_inc(zeros_ready, 1)
            pool.wait_ge(zeros_ready, 1)
            pool.wait_ge(x_in_dma[2], 32)
            regroup_channel(pool.tensor_copy, 2).then_inc(x_by_col_ready[2], 1)
            pool.memset(qk_pad[:, :, :, HD:HPAD], 0.0).then_inc(pads_zeroed, 1)
            pool.memset(v_bd[:, :, :, :], 0.0).then_inc(pads_zeroed, 1)
            pool.memset(att[:, :, D:XW], 0.0).then_inc(pads_zeroed, 1)
            pool.wait_ge(pads_zeroed, 3)
            for par in range(2):
                pool.memset(v_bd[par * SEQ:(par + 1) * SEQ, :, :, par * VW + HD:par * VW + HD + 1], 1.0).then_inc(pads_zeroed, 1)
            pool.wait_ge(pads_zeroed, 5)
            pool.wait_ge(attn0_dma, 16 * ATTN0_LOADS)
            for a in range(2):
                if a == 1:
                    pool.wait_ge(attn1_dma, 16 * ATTN1_LOADS)
                    h_round = 2
                else:
                    h_round = 0
                for t in range(NT):
                    pool.wait_ge(h_ready, h_round * NT + t + 1)
                    pool.tensor_tensor(hb[:, t], h[:, t], bo[a][:, :], ALU.add).then_inc(hb_ready, 1)
                if a == 0:
                    for t in range(NT):
                        pool.wait_ge(feat_exp, t + 1)
                        pool.tensor_scalar(qk_pad[:, t, :, 0:HD], fexp[:, t], RFM_EPS, 1.0, ALU.add, ALU.mult).then_inc(qk_pad_ready, 1)
                    pool.wait_ge(zeros_dma, 32)
                    pool.wait_ge(xn_ready, 2 * NT)
                    pool.wait_ge(slots_ready, 1)
                    for k in range(PICKS):
                        for t in range(NT):
                            pool.indirect_dma_start(out=x_slots, out_offset=bass.IndirectOffsetOnAxis(ap=pick_slot_u[:, k * NT + t:k * NT + t + 1], axis=0),
                                                    in_=xn[:, t, :], in_offset=None).then_inc(scatter_dma, 16)
                    pool.wait_ge(y_stored, 1)
                    for t in range(NT):
                        for k in range(PICKS):
                            pool.indirect_dma_start(out=y_back[:, t, k], out_offset=None, in_=y_slots,
                                                    in_offset=bass.IndirectOffsetOnAxis(ap=pick_slot_u[:, k * NT + t:k * NT + t + 1], axis=0)).then_inc(y_back_dma[t], 16)
                else:
                    for t in range(NT):
                        pool.wait_ge(qk_biased, t + 1)
                        pool.tensor_tensor(fexp[:, t].rearrange("p h f -> p (h f)").rearrange("p (m n) -> p m n", m=2),
                                           turned[:, t].rearrange("p (m n) -> p m n", m=2),
                                           const("rope_cos").unsqueeze(1).to_broadcast([P, 2, D]), ALU.mult).then_inc(rope_cos_part, 1)

        @block.scalar
        def _(act):
            load_columns_t = dram["L0_tok_W"]
            act.dma_start(wtok[:, 0, :], load_columns_t[0:DA, :]).then_inc(wtok_dma, 16)
            act.dma_start(wtok[0:DB, 1, :], load_columns_t[DA:D, :]).then_inc(wtok_dma, 16)
            act.dma_start(cst[:, :], consts).then_inc(const_dma, 16)
            load_row(act, btok[:, :], dram["L0_tok_b"], attn0_dma)
            load_columns(act, wqkv0, dram["L0_attn_w_inp"][0], attn0_dma)
            act.dma_start(bqk0[:, :], dram["L0_attn_b_inp"][0:2 * D].rearrange("(c p) -> p c", p=P), allow_slow_non_contiguous=True).then_inc(attn0_dma, 16)
            load_bv(act, bv[0], dram["L0_attn_b_inp"][2 * D:3 * D], attn0_dma)
            act.dma_start(omega8[:, :, :], dram["L0_attn_omega"].unsqueeze(1).to_broadcast([HD, P // HD, HD])).then_inc(attn0_dma, 16)
            load_columns(act, wo[0], dram["L0_attn_w_out"][0], attn0_dma)
            load_row(act, bo[0], dram["L0_attn_b_out"], attn0_dma)

            def turned_tokens(r):
                act.wait_ge(moments, (r + 1) * NT)
                act.activation(rstd[:, :, 0], mv[:, :, 1], ACT.Sqrt, bias=const("ln_eps")).then_inc(deviation, 1)
                for t in range(NT):
                    act.wait_ge(xnT_mm, r * NT + t + 1)
                    act.copy(xnT[:, :, t * P:(t + 1) * P], ps[:, 2 * t + 1, 0:2 * P].rearrange("p (c n) -> p c n", c=2)).then_inc(xnT_sb, 1)

            act.wait_ge(x_in_dma[1], 32)
            regroup_channel(act.copy, 1).then_inc(x_by_col_ready[1], 1)
            for n in range(0, 2 * NCH, 2):
                act.wait_ge(patches_mm, n + 1)
                patch_job(act.copy, n).then_inc(patches_act, 1)
            turned_tokens(0)
            act.wait_ge(attn0_dma, 16 * ATTN0_LOADS)
            for c in range(3):
                act.wait_ge(qkT0_mm, c + 1)
                act.activation(qkT0[:, c, :], ps[:, c, :], ACT.Identity, bias=bqk0[:, c:c + 1]).then_inc(qkT0_sb, 1)
            for t in range(NT):
                act.wait_ge(feat_centred, t + 1)
                act.activation(fexp[:, t].rearrange("p h f -> p (h f)"), turned[:, t], ACT.Exp).then_inc(feat_exp, 1)

            def attention(a):
                for t in range(NT):
                    act.wait_ge(qk_padT_mm, NT * a + t + 1)
                    bank = 4 + 2 * (t % 2)
                    act.copy(qk_padT[:, t].rearrange("p (b j) n -> p b (j n)", b=2), ps[:, bank:bank + 2, 0:HB * P]).then_inc(qk_padT_sb, 1)
                if a == 1:
                    for t in range(NT):
                        act.wait_ge(centred, t + 1)
                        act.activation(probs[:, t].rearrange("p h k -> p (h k)"), probs[:, t].rearrange("p h k -> p (h k)"),
                                       ACT.Exp, scale=float(HD) ** -0.5).then_inc(probs_exp, 1)
                for t in range(NT):
                    act.wait_ge(probsT_mm, NT * a + t + 1)
                    act.copy(probsT[:, t].rearrange("p (b j) n -> p b (j n)", b=2), ps[:, 2 * t:2 * t + 2, 0:NPAIR // 2 * P]).then_inc(probsT_sb, 1)
                for t in range(NT):
                    act.wait_ge(attT_mm, NT * a + t + 1)
                    act.copy(attT[:, t], ps[:, 2 * t + 1, 0:2 * P].rearrange("p (c n) -> p c n", c=2)).then_inc(attT_sb, 1)

            attention(0)
            turned_tokens(1)
            act.wait_ge(gates_centred, 2)
            act.activation(gate_in[:, :], gate_in[:, :], ACT.Exp).then_inc(gates_exp, 1)
            act.wait_ge(ov_mm, 1)
            act.copy(b1T[:, :, :].rearrange("p c e -> p (c e)"), ps[:, 5, 0:KH * NE]).then_inc(b1T_sb, 1)
            act.copy(b1T_ov[:, :, :].rearrange("p c e -> p (c e)"), ps[:, 5, 256:256 + KH * NOV]).then_inc(b1T_sb, 1)
            act.copy(ov_info[0:1, 0:NOV], ps[0:1, 5, 384:384 + NOV]).then_inc(ov_info_ready, 1)
            act.wait_ge(combT_mm, 1)
            act.copy(combT[:, :], ps[0:NE, 1, 0:TOK]).then_inc(combT_sb, 1)
            act.wait_ge(b1T_sb, 2)

            def gelu(bank, buf, bias, done):
                for c in range(KH):
                    last = act.activation(hidden[:, buf, c, :], ps[:, bank + c // 3, (c % 3) * P:(c % 3 + 1) * P], ACT.Gelu, bias=bias(c))
                last.then_inc(done, 1)

            def gelus(i):
                for u in range(RING):
                    e = i * RING + u
                    act.wait_ge(up_mm, e + 1)
                    gelu(2 + 2 * (u % 2), u % 2, lambda c: b1T[:, c, bass.ds(e, 1)], gelu_done)

            with act.Fori(0, ROUNDS) as i:
                gelus(i)
            act.wait_ge(ov_info_ready, 2)
            tiles = act.value_load(ov_info[0:1, NOV:NOV + 1], min_val=0, max_val=NOV)
            with act.Fori(0, NOV) as i:
                with act.If(tiles > i):
                    act.wait_ge(ov_up_mm, i + 1)
                    gelu(2, 0, lambda c: b1T_ov[:, c, bass.ds(i, 1)], ov_gelu)
                act.nop()
            for e in range(N1):
                act.wait_ge(ffn_wT_mm, e + 1)
                bank = 2 * (e % 4)
                act.copy(w13T[:, e].rearrange("p m i -> p (m i)"), ps[:, bank, 0:2 * P]).then_inc(ffn_wT_sb, 1)
                act.copy(w13T_tail[:, e], ps[:, bank, 2 * P:3 * P]).then_inc(ffn_wT_sb, 1)
                act.copy(w2T[:, e], ps[:, bank + 1, 0:D]).then_inc(ffn_wT_sb, 1)
            act.wait_ge(ffn_wT_mm, N1 + 1)
            act.copy(gate_wT[:, :, :].rearrange("p c e -> p (c e)"), ps[:, 2, 0:2 * E1]).then_inc(ffn_wT_sb, 1)
            turned_tokens(2)
            attention(1)
            turned_tokens(3)
            act.wait_ge(gate_mm, 1)
            act.activation(score[:, :, :].rearrange("p t e -> p (t e)"), ps[:, 4, 0:NT * E1], ACT.Sigmoid).then_inc(score_ready, 1)

            def silus(n, u, first=False):
                act.wait_ge(up1_mm, n + 1)
                if not first:
                    act.wait_ge(gated_ready, n - 1)
                act.activation(silu[:, u, :], ps[:, 2 * u, :], ACT.Silu).then_inc(silu_done, 1)

            silus(0, 0, True)
            silus(1, 1, True)
            silus(2, 0)
            with act.Fori(1, N1 // 2) as i:
                silus(2 * i + 1, 1)
                silus(2 * i + 2, 0)

        @block.tensor
        def _(pe):
            pe.wait_ge(const_dma, 16)
            pe.wait_ge(wtok_dma, 32)
            for k in range(KP):
                o = (k % 2) * D
                nc.tensor.transpose(ps[:, k // 2, o:o + DA], wtok[:, 0, k * P:(k + 1) * P], ident)
                nc.tensor.transpose(ps[:, k // 2, o + DA:o + D], wtok[0:DB, 1, k * P:(k + 1) * P], ident[0:DB, 0:DB]).then_inc(wtokT_mm, 1)
            for n in range(2 * NCH):
                c, part = n // 2, n % 2
                if part == 0:
                    pe.wait_ge(x_by_col_ready[c], 1)
                if n == 5:
                    pe.wait_ge(patches_act, 1)
                for w in range(4):
                    last = nc.tensor.transpose(ps[:, PATCH_BANK[n], w * P:(w + 1) * P], x_by_col[:, c, part * 4 + w], ident)
                last.then_inc(patches_mm, 1)
            pe.wait_ge(wtokT_sb, KP // 2)
            pe.wait_ge(patches_act, NCH)
            pe.wait_ge(patches_dve, NCH)
            for t in range(NT):
                if t == 3:
                    pe.wait_ge(h_ready, 1)
                for k in range(KP):
                    last = nc.tensor.matmul(ps[:, t % 3, 0:D], patchesT[:, k, t * P:(t + 1) * P], wtokT[:, k, :],
                                            start=(k == 0), stop=(k == KP - 1))
                last.then_inc(embed_mm, 1)

            def turn_tokens(r):
                for t in range(NT):
                    pe.wait_ge(xn_ready, r * NT + t + 1)
                    for c in range(2):
                        last = nc.tensor.transpose(ps[:, 2 * t + 1, c * P:(c + 1) * P], xn[:, t, c * P:(c + 1) * P], ident)
                    last.then_inc(xnT_mm, 1)

            def values(wv):
                w = wv.rearrange("p c (j q d) -> p c q j d", q=2, d=HD)
                for b in range(NIMG):
                    for q in range(2):
                        dst = ps[q * SEQ:(q + 1) * SEQ, 6 + b // 4, (b % 4) * (D // 2):(b % 4 + 1) * (D // 2)]
                        for c, rows in ((0, DA), (1, DB)):
                            last = nc.tensor.matmul(dst, xnT[0:rows, c, b * SEQ:(b + 1) * SEQ], w[0:rows, c, q],
                                                    start=(c == 0), stop=(c == 1))
                    if b % 4 == 3:
                        last.then_inc(v_mm, 1)

            def attention(a):
                for t in range(NT):
                    pe.wait_ge(qk_pad_ready, NT * a + t + 1)
                    if t == 1:
                        pe.wait_ge(v_sb, 4 * (a + 1))
                    if t >= 2:
                        pe.wait_ge(qk_padT_sb, NT * a + t - 1)
                    for j in range(2 * HB):
                        last = nc.tensor.transpose(ps[:, 4 + 2 * (t % 2) + j // HB, (j % HB) * P:(j % HB + 1) * P],
                                                   qk_pad[:, t].rearrange("p h f -> p (h f)")[:, j * P:(j + 1) * P], ident)
                    last.then_inc(qk_padT_mm, 1)
                for t in range(NT):
                    if t == 0:
                        pe.wait_ge(qk_padT_sb, NT * a + 1)
                    if t == 1:
                        pe.wait_ge(qk_padT_sb, NT * a + NT)
                    if t >= 2:
                        pe.wait_ge(scores_read, NT * a + t - 1)
                    for i in range(HG):
                        for j in range(HB):
                            for b in range(IPT):
                                rows, cols = slice(i * HPAD, i * HPAD + HD), slice(b * SEQ, (b + 1) * SEQ)
                                last = nc.tensor.matmul(ps[b * SEQ:(b + 1) * SEQ, 4 * (t % 2) + i, j * SEQ:(j + 1) * SEQ],
                                                        qk_padT[rows, t, j, cols], qk_padT[rows, t, HB + j, cols], start=True, stop=True)
                    last.then_inc(scores_mm, 1)
                for t in range(NT):
                    pe.wait_ge(scores_read, NT * a + (3 if t < 2 else 4))
                    if a == 1:
                        pe.wait_ge(probs_exp, t + 1)
                    for j in range(NPAIR):
                        last = nc.tensor.transpose(ps[:, 2 * t + j // 3, (j % 3) * P:(j % 3 + 1) * P],
                                                   probs[:, t, 2 * j:2 * j + 2, :].rearrange("p h k -> p (h k)"), ident)
                    last.then_inc(probsT_mm, 1)
                pe.wait_ge(v_sb, 4 * (a + 1))
                for t in range(NT):
                    pe.wait_ge(probsT_sb, NT * a + t + 1)
                    for b in range(IPT):
                        for j in range(NPAIR):
                            last = nc.tensor.matmul(ps[b * SEQ:(b + 1) * SEQ, 2 * t, j * 2 * VW:(j + 1) * 2 * VW],
                                                    probsT[:, t, j, b * SEQ:(b + 1) * SEQ], v_bd[:, IPT * t + b, j, :], start=True, stop=True)
                    last.then_inc(att_mm, 1)
                for t in range(NT):
                    pe.wait_ge(att_ready, NT * a + t + 1)
                    for c in range(2):
                        last = nc.tensor.transpose(ps[:, 2 * t + 1, c * P:(c + 1) * P], att[:, t, c * P:(c + 1) * P], ident)
                    last.then_inc(attT_mm, 1)
                for t in range(NT):
                    pe.wait_ge(attT_sb, NT * a + t + 1)
                    for c, rows in ((0, DA), (1, DB)):
                        last = nc.tensor.matmul(ps[:, 2 * t, 0:D], attT[0:rows, t, c, :], wo[a][0:rows, c, :], start=(c == 0), stop=(c == 1))
                    last.then_inc(proj_mm, 1)

            turn_tokens(0)
            pe.wait_ge(attn0_dma, 16 * ATTN0_LOADS)
            pe.wait_ge(xnT_sb, NT)
            for c in range(3):
                for k, rows in ((0, DA), (1, DB)):
                    last = nc.tensor.matmul(ps[:, c, :], wqkv0[0:rows, k, c * P:(c + 1) * P], xnT[0:rows, k, :], start=(k == 0), stop=(k == 1))
                last.then_inc(qkT0_mm, 1)
            values(wqkv0[:, :, 2 * D:3 * D])
            nc.tensor.transpose(ps[:, 3, 0:HD], omega8[:, :, :].rearrange("f h d -> f (h d)"), ident[0:HD, 0:HD]).then_inc(omega_mm, 1)
            pe.wait_ge(omega_sb, 1)
            pe.wait_ge(qkT0_sb, 3)
            for t in range(NT):
                for c in range(3):
                    last = nc.tensor.matmul(ps[:, t, c * P:(c + 1) * P], qkT0[:, c, t * P:(t + 1) * P], omega_bd[:, :], start=True, stop=True)
                last.then_inc(qk_mm, 1)
            attention(0)
            turn_tokens(1)
            pe.wait_ge(route_dma, 16 * ROUTE_LOADS)
            for t in range(NT):
                pe.wait_ge(xnT_sb, NT + t + 1)
                for k, rows in ((0, DA), (1, DB)):
                    last = nc.tensor.matmul(ps[:, 0, t * (G + NE):(t + 1) * (G + NE)], xnT[0:rows, k, t * P:(t + 1) * P], wroute[0:rows, k, :],
                                            start=(k == 0), stop=(k == 1))
            last.then_inc(logits_mm, 1)
            for c in range(KH):
                nc.tensor.transpose(ps[:, 5, c * NE:(c + 1) * NE], b1_rows[:, c * P:(c + 1) * P], ident[0:NE, 0:NE])
            pe.wait_ge(chosen_ready, 1)
            for t in range(NT + 1):
                for s in range(min(t + 1, NT)):
                    nc.tensor.matmul(ps[:, 2, t * NE:(t + 1) * NE], const("before") if s == t else const("ones"), chosen[:, s, :],
                                     start=(s == 0), stop=(s == min(t, NT - 1)))
            for t in range(NT):
                last = nc.tensor.matmul(ps[0:NE, 3, 0:1], chosen[:, t, :], const("ones", P, 1), start=(t == 0), stop=(t == NT - 1))
            last.then_inc(counts_mm, 1)
            pe.wait_ge(extra_col_ready, 1)
            nc.tensor.matmul(ps[0:NE, 4, 0:1], const("before", NE, NE), extra_col[:, :], start=True, stop=True).then_inc(extra_at_mm, 1)
            pe.wait_ge(ov_onehot_ready, 1)
            for c in range(KH):
                nc.tensor.matmul(ps[:, 5, 256 + c * NOV:256 + (c + 1) * NOV], b1_rows[:, c * P:(c + 1) * P], ov_onehot[:, :], start=True, stop=True)
            nc.tensor.matmul(ps[0:1, 5, 384:384 + NOV], const("row", NE), ov_onehot[:, :], start=True, stop=True).then_inc(ov_mm, 1)
            pe.wait_ge(comb_ready, 1)
            for t in range(NT):
                last = nc.tensor.transpose(ps[0:NE, 1, t * P:(t + 1) * P], comb[:, t, :], ident)
            last.then_inc(combT_mm, 1)
            pe.wait_ge(combT_sb, 1)
            for t in range(NT):
                last = nc.tensor.matmul(ps[:, 6 + t // 2, (t % 2) * D:(t % 2 + 1) * D], combT[:, t * P:(t + 1) * P], b2_rows[:, :], start=True, stop=True)
            last.then_inc(b2_mm, 1)

            def turn_rows(u, buf, done):
                for c in range(2):
                    last = nc.tensor.transpose(ps[:, buf, c * P:(c + 1) * P], x_rows[:, u, c * P:(c + 1) * P], ident)
                last.then_inc(done, 1)

            def up(u, buf, done):
                for c in range(KH // 2):
                    for half in range(2):
                        nc.tensor.matmul(ps[:, 2 + 2 * buf + half, c * P:(c + 1) * P], w1[:, u, (c + 3 * half) * P:(c + 3 * half + 1) * P],
                                         x_rowsT[:, buf, 0, :], start=True, stop=False)
                    for half in range(2):
                        rows = slice(half * DB, (half + 1) * DB)
                        last = nc.tensor.matmul(ps[:, 2 + 2 * buf + half, c * P:(c + 1) * P], w1_tail[rows, u, c * P:(c + 1) * P],
                                                x_rowsT[rows, buf, 1, :], start=False, stop=True)
                last.then_inc(done, 1)

            def down(u, buf, done):
                for c in range(KH):
                    last = nc.tensor.matmul(ps[:, 6 + buf, 0:D], hidden[:, buf, c, :], w2[:, u, c, :], start=(c == 0), stop=(c == KH - 1))
                last.then_inc(done, 1)

            def rows_in(i, u):
                pe.wait_ge(x_dma[u], 16 * (i + 1))
                turn_rows(u, u % 2, rowsT_mm)

            def up_in(i, u):
                pe.wait_ge(w_dma[u], 16 * W_LOADS * (i + 1))
                pe.wait_ge(rowsT_sb, i * RING + u + 1)
                up(u, u % 2, up_mm)

            def experts(i, first, last_round):
                for u in range(RING):
                    if not (last_round and u + 1 >= RING):
                        up_in(i + (u + 1) // RING, (u + 1) % RING)
                    if not (last_round and u + 2 >= RING):
                        rows_in(i + (u + 2) // RING, (u + 2) % RING)
                    pe.wait_ge(gelu_done, i * RING + u + 1)
                    if not (first and u < 2):
                        pe.wait_ge(y_ready, i * RING + u - 1)
                    down(u, u % 2, down_mm)

            rows_in(0, 0)
            rows_in(0, 1)
            pe.wait_ge(b1T_sb, 2)
            up_in(0, 0)
            pe.wait_ge(b2_added, 2)
            experts(0, True, False)
            with pe.Fori(1, ROUNDS - 1) as i:
                experts(i, False, False)
            experts(ROUNDS - 1, False, True)
            pe.wait_ge(y_ready, NE)
            pe.wait_ge(ov_info_ready, 2)
            tiles = pe.value_load(ov_info[0:1, NOV:NOV + 1], min_val=0, max_val=NOV)
            with pe.Fori(0, NOV) as i:
                with pe.If(tiles > i):
                    pe.wait_ge(ov_x_dma, 16 * (i + 1))
                    turn_rows(0, 0, ov_rowsT_mm)
                    pe.wait_ge(ov_w_dma, 16 * W_LOADS * (i + 1))
                    pe.wait_ge(ov_rowsT_sb, i + 1)
                    up(0, 0, ov_up_mm)
                    pe.wait_ge(ov_gelu, i + 1)
                    down(0, 0, ov_down_mm)
                    pe.wait_ge(ov_y_ready, i + 1)
                pe.nop()
            pe.wait_ge(ffn_dma, 16 * FFN_LOADS)
            for e in range(N1):
                if e >= 4:
                    pe.wait_ge(ffn_wT_sb, 3 * (e - 3))
                bank = 2 * (e % 4)
                for m in range(2):
                    nc.tensor.transpose(ps[:, bank, m * P:(m + 1) * P], w13_raw[:, e, m, :], ident)
                nc.tensor.transpose(ps[:, bank, 2 * P:3 * P], w13_raw_tail[:, e, :], ident)
                nc.tensor.transpose(ps[:, bank + 1, 0:DA], w2_raw[:, e, :], ident)
                nc.tensor.transpose(ps[:, bank + 1, DA:D], w2_raw_tail[:, e, :], ident[0:DB, 0:DB]).then_inc(ffn_wT_mm, 1)
            pe.wait_ge(ffn_wT_sb, 3 * (N1 - 3))
            for c in range(2):
                last = nc.tensor.transpose(ps[:, 2, c * E1:(c + 1) * E1], gate_rows[:, c * P:(c + 1) * P], ident[0:E1, 0:E1])
            last.then_inc(ffn_wT_mm, 1)
            pe.wait_ge(ffn_wT_sb, 3 * N1 + 1)
            turn_tokens(2)
            pe.wait_ge(attn1_dma, 16 * ATTN1_LOADS)
            for t in range(NT):
                pe.wait_ge(xnT_sb, 2 * NT + (NT if t == 3 else t + 1))
                for k, rows in ((0, DA), (1, DB)):
                    last = nc.tensor.matmul(ps[:, t, 0:2 * D], xnT[0:rows, k, t * P:(t + 1) * P], wqkv1[0:rows, k, 0:2 * D], start=(k == 0), stop=(k == 1))
                last.then_inc(qk_mm, 1)
            values(wqkv1[:, :, 2 * D:3 * D])
            attention(1)
            turn_tokens(3)
            for t in range(NT):
                pe.wait_ge(xnT_sb, 3 * NT + t + 1)
                for k, rows in ((0, DA), (1, DB)):
                    last = nc.tensor.matmul(ps[:, 4, t * E1:(t + 1) * E1], xnT[0:rows, k, t * P:(t + 1) * P], gate_wT[0:rows, k, :], start=(k == 0), stop=(k == 1))
            last.then_inc(gate_mm, 1)

            def up1(n, u, first=False):
                if not first:
                    pe.wait_ge(gated_ready, n - 1)
                w, wt = w13T[:, n], w13T_tail[:, n]
                for m in range(2):
                    nc.tensor.matmul(ps[:, 2 * u + m, :], w[:, m, :], xnT[:, 0, :], start=True, stop=False)
                for m in range(2):
                    rows = slice(m * DB, (m + 1) * DB)
                    last = nc.tensor.matmul(ps[:, 2 * u + m, :], wt[rows, :], xnT[rows, 1, :], start=False, stop=True)
                last.then_inc(up1_mm, 1)

            def down1(n, u, first=False):
                pe.wait_ge(gated_ready, n + 1)
                if not first:
                    pe.wait_ge(summed, n - 1)
                w = w2T[:, n]
                for t in range(NT):
                    last = nc.tensor.matmul(ps[:, 6 - 2 * u + t // 2, (t % 2) * D:(t % 2 + 1) * D], gated[:, u, t * P:(t + 1) * P], w, start=True, stop=True)
                last.then_inc(down1_mm, 1)

            up1(0, 0, True)
            up1(1, 1, True)
            down1(0, 0, True)
            pe.wait_ge(score_ready, 1)
            up1(2, 0)
            down1(1, 1, True)
            for i in range(1, N1 // 2):
                up1(2 * i + 1, 1)
                down1(2 * i, 0)
                up1(2 * i + 2, 0)
                down1(2 * i + 1, 1)
            down1(N1 - 1, 0)

        @block.vector
        def _(dve):
            steps = [0]

            def step(ins):
                steps[0] += 1
                ins.then_inc(dve_step, 1)
                return steps[0]

            def after(n):
                dve.wait_ge(dve_step, n)

            def layer_norm(r):
                for t in range(NT):
                    dve.wait_ge(h_ready, r * NT + t + 1)
                    n = step(dve.bn_stats(stats[:, t], h[:, t]))
                after(n)
                for t in range(NT):
                    dve.bn_aggr(mv[:, t], stats[:, t]).then_inc(moments, 1)
                dve.wait_ge(deviation, r + 1)
                after(step(dve.reciprocal(rstd[:, :, 0], rstd[:, :, 0])))
                for t in range(NT):
                    n = step(dve.tensor_scalar(xn[:, t, 0:D], h[:, t], mv[:, t, 0:1], rstd[:, t], ALU.subtract, ALU.mult))
                    after(n)
                    dve.tensor_copy(xn[:, t, D:XW], xn[:, t, DA:D]).then_inc(xn_ready, 1)

            def values_out(a):
                for g in range(2):
                    dve.wait_ge(v_mm, 2 * a + g + 1)
                    for q in range(2):
                        rows = slice(q * SEQ, (q + 1) * SEQ)
                        dve.tensor_tensor(v_bd[rows, 4 * g:4 * g + 4, :, q * VW:q * VW + HD],
                                          ps[rows, 6 + g, 0:2 * D].rearrange("p (b j d) -> p b j d", b=4, d=HD),
                                          bv[a][rows, :].rearrange("p (j d) -> p j d", d=HD).unsqueeze(1).to_broadcast([SEQ, 4, NPAIR, HD]),
                                          ALU.add).then_inc(v_sb, 1)

            def attention(a):
                for t in range(NT):
                    dve.wait_ge(scores_mm, NT * a + t + 1)
                    src = ps[:, 4 * (t % 2):4 * (t % 2) + 4, 0:HB * SEQ].rearrange("p i (j k) -> p i j k", j=HB)
                    dst = probs[:, t].rearrange("p (j i) k -> p i j k", i=HG)
                    mask = const("future" if a else "causal").unsqueeze(1).unsqueeze(1).to_broadcast([P, HG, HB, SEQ])
                    dve.tensor_tensor(dst, src, mask, ALU.add if a else ALU.mult).then_inc(scores_read, 1)
                    if a == 1:
                        dve.wait_ge(scores_read, NT * a + t + 1)
                        after(step(dve.tensor_reduce(rowmax[:, t], probs[:, t], X, ALU.max)))
                        dve.tensor_tensor(probs[:, t], probs[:, t], rowmax[:, t].unsqueeze(2).to_broadcast([P, H, SEQ]), ALU.subtract).then_inc(centred, 1)
                for t in range(NT):
                    dve.wait_ge(att_mm, NT * a + t + 1)
                    o = ps[:, 2 * t, 0:H * VW].rearrange("p (h c) -> p h c", c=VW)
                    if a == 0:
                        after(step(dve.tensor_scalar(rden[:, t], o[:, :, HD], RFM_EPS * HD, None, ALU.add)))
                        after(step(dve.reciprocal(rden[:, t], rden[:, t])))
                    else:
                        after(step(dve.reciprocal(rden[:, t], o[:, :, HD])))
                    dve.tensor_tensor(att[:, t, 0:D].rearrange("p (h c) -> p h c", c=HD), o[:, :, 0:HD],
                                      rden[:, t].unsqueeze(2).to_broadcast([P, H, HD]), ALU.mult).then_inc(att_ready, 1)
                for t in range(NT):
                    dve.wait_ge(proj_mm, NT * a + t + 1)
                    dve.wait_ge(hb_ready, NT * a + t + 1)
                    dve.tensor_tensor(h[:, t], ps[:, 2 * t, 0:D], hb[:, t], ALU.add).then_inc(h_ready, 1)

            dve.wait_ge(x_in_dma[0], 32)
            regroup_channel(dve.tensor_copy, 0).then_inc(x_by_col_ready[0], 1)
            for c in range(KP // 2):
                dve.wait_ge(wtokT_mm, 2 * c + 2)
                dve.tensor_copy(wtokT[:, 2 * c:2 * c + 2, :].rearrange("p k e -> p (k e)"), ps[:, c, 0:2 * D]).then_inc(wtokT_sb, 1)
            for n in range(1, 2 * NCH, 2):
                dve.wait_ge(patches_mm, n + 1)
                patch_job(dve.tensor_copy, n).then_inc(patches_dve, 1)
            dve.wait_ge(attn0_dma, 16 * ATTN0_LOADS)
            for t in range(NT):
                dve.wait_ge(embed_mm, t + 1)
                dve.tensor_tensor(h[:, t], ps[:, t % 3, 0:D], btok[:, :], ALU.add).then_inc(h_ready, 1)
            layer_norm(0)
            dve.wait_ge(pads_zeroed, 5)
            values_out(0)
            dve.wait_ge(omega_mm, 1)
            dve.tensor_tensor(omega_bd[:, :].rearrange("p (h f) -> p h f", f=HD),
                              ps[:, 3, 0:HD].unsqueeze(1).to_broadcast([P, P // HD, HD]),
                              const("headblock").unsqueeze(2).to_broadcast([P, P // HD, HD]), ALU.mult).then_inc(omega_sb, 1)
            for t in range(NT):
                dve.wait_ge(qk_mm, t + 1)
                s = ps[:, t, 0:2 * D].rearrange("p (h f) -> p h f", f=HD)
                step(dve.tensor_reduce(fsum[:, t], s, X, ALU.add))
                step(dve.tensor_reduce(foff[:, t, 0:H], s[:, 0:H], X, ALU.max))
                after(step(dve.tensor_reduce(fmax[:, t], ps[:, t, D:2 * D], X, ALU.max)))
                step(dve.scalar_tensor_tensor(out=foff[:, t, 0:H], in0=fsum[:, t, 0:H], scalar=0.5, in1=foff[:, t, 0:H], op0=ALU.mult, op1=ALU.add))
                after(step(dve.tensor_scalar(foff[:, t, H:2 * H], fsum[:, t, H:2 * H], 0.5, fmax[:, t], ALU.mult, ALU.add)))
                dve.tensor_tensor(turned[:, t].rearrange("p (h f) -> p h f", f=HD), s,
                                  foff[:, t].unsqueeze(2).to_broadcast([P, 2 * H, HD]), ALU.subtract).then_inc(feat_centred, 1)
            attention(0)
            layer_norm(1)
            dve.wait_ge(route_dma, 16 * ROUTE_LOADS)
            dve.wait_ge(logits_mm, 1)
            lg = ps[:, 0, 0:NT * (G + NE)].rearrange("p (t c) -> p t c", t=NT)
            step(dve.tensor_tensor(ggl[:, :, :], lg[:, :, 0:G], broute[:, 0:G].unsqueeze(1).to_broadcast([P, NT, G]), ALU.add))
            after(step(dve.tensor_tensor(gel[:, :, :].rearrange("p (t g) e -> p t (g e)", t=NT), lg[:, :, G:G + NE],
                                         broute[:, G:G + NE].unsqueeze(1).to_broadcast([P, NT, NE]), ALU.add)))

            def ranks(dst, v, groups, n, tie):
                b = beats[:, 0:groups * n * n].rearrange("p (a i j) -> p a i j", a=groups, i=n)
                q = ties[:, 0:groups * n * n].rearrange("p (a i j) -> p a i j", a=groups, i=n)
                other = v.unsqueeze(2).to_broadcast([P, groups, n, n])
                own = v.unsqueeze(3).to_broadcast([P, groups, n, n])
                after(step(dve.tensor_tensor(q, other, own, ALU.is_equal)))
                qf = q.rearrange("p a i j -> p a (i j)")
                step(dve.tensor_tensor(qf, qf, const(tie).unsqueeze(1).to_broadcast([P, groups, n * n]), ALU.mult))
                after(step(dve.tensor_tensor(b, other, own, ALU.is_gt)))
                after(step(dve.tensor_tensor(b, b, q, ALU.add)))
                after(step(dve.tensor_reduce(dst, b, X, ALU.add)))

            ranks(rank_g[:, :, :], ggl[:, :, :], NT, G, "tie4")
            ranks(rank_e[:, :, :], gel[:, :, :], NT * G, EG, "tie8")
            step(dve.tensor_scalar(sel_g[:, :, :], rank_g[:, :, :], 1.5, None, ALU.is_lt))
            after(step(dve.tensor_scalar(sel_e[:, :, :], rank_e[:, :, :], 1.5, None, ALU.is_lt)))
            sel_gf = sel_g[:, :, :].rearrange("p t g -> p (t g)")
            dve.tensor_tensor(chosen[:, :, :].rearrange("p t (g e) -> p (t g) e", g=G), sel_e[:, :, :],
                              sel_gf.unsqueeze(2).to_broadcast([P, NT * G, EG]), ALU.mult).then_inc(chosen_ready, 1)
            gg = gate_g.rearrange("p (t g) -> p t g", t=NT)
            ge = gate_e.rearrange("p (a e) -> p a e", e=EG)
            step(dve.tensor_reduce(top[:, 0:NT], ggl[:, :, :], X, ALU.max))
            after(step(dve.tensor_reduce(top[:, NT:], gel[:, :, :], X, ALU.max)))
            dve.tensor_tensor(gg, ggl[:, :, :], top[:, 0:NT].unsqueeze(2).to_broadcast([P, NT, G]), ALU.subtract).then_inc(gates_centred, 1)
            dve.tensor_tensor(ge, gel[:, :, :], top[:, NT:].unsqueeze(2).to_broadcast([P, NT * G, EG]), ALU.subtract).then_inc(gates_centred, 1)
            for r in range(2):
                step(dve.tensor_scalar(pick_g[:, r], rank_g[:, :, :], float(r), None, ALU.is_equal))
                after(step(dve.tensor_scalar(pick_e[:, r].rearrange("p t (g e) -> p (t g) e", g=G), rank_e[:, :, :], float(r), None, ALU.is_equal)))
            for k in range(PICKS):
                n = step(dve.tensor_tensor(pick[:, k].rearrange("p t (g e) -> p (t g) e", g=G),
                                           pick_e[:, k % 2].rearrange("p t (g e) -> p (t g) e", g=G),
                                           pick_g[:, k // 2].rearrange("p t g -> p (t g)").unsqueeze(2).to_broadcast([P, NT * G, EG]), ALU.mult))
            after(n)
            dve.wait_ge(counts_mm, 1)
            count, place = ps[:, 2, NT * NE:(NT + 1) * NE], ps[:, 2, 0:NT * NE].rearrange("p (t e) -> p t e", t=NT)
            for dst, src, done in ((extra_col[:, :], ps[0:NE, 3, 0:1], extra_col_ready), (extra[:, :], count, None)):
                after(step(dve.tensor_scalar(dst, src, float(P), None, ALU.is_gt)))
                for m in range(2, NT):
                    ins = dve.scalar_tensor_tensor(out=dst, in0=src, scalar=float(m * P), in1=dst, op0=ALU.is_gt, op1=ALU.add)
                    if done is not None and m == NT - 1:
                        ins.then_inc(done, 1)
                    else:
                        after(step(ins))
            after(step(dve.tensor_tensor_scan(extra_sum[:, :], const("ones", P, NE), extra[:, :], 0.0, ALU.mult, ALU.add)))
            dve.tensor_copy(ov_info[0:1, NOV:NOV + 1], extra_sum[0:1, NE - 1:NE]).then_inc(ov_info_ready, 1)
            after(step(dve.tensor_tensor(shift[:, :], extra_sum[:, :], extra[:, :], ALU.subtract)))
            after(step(dve.tensor_scalar(shift[:, :], shift[:, :], float(P), float((NE - 1) * P), ALU.mult, ALU.add)))
            after(step(dve.tensor_tensor(shift[:, :], shift[:, :], const("first_slot"), ALU.subtract)))
            after(step(dve.scalar_tensor_tensor(out=slot[:, :, :], in0=place, scalar=float(P) - 0.5, in1=shift[:, :].unsqueeze(1).to_broadcast([P, NT, NE]),
                                                op0=ALU.is_gt, op1=ALU.mult)))
            after(step(dve.tensor_tensor(slot[:, :, :], place, slot[:, :, :], ALU.add)))
            after(step(dve.tensor_tensor(slot[:, :, :], slot[:, :, :], const("first_slot").unsqueeze(1).to_broadcast([P, NT, NE]), ALU.add)))

            def take(dst, values):
                after(step(dve.tensor_tensor(picked[:, :, :].rearrange("p (k t) e -> p k (t e)", k=PICKS),
                                             pick[:, :, :, :].rearrange("p k t e -> p k (t e)"),
                                             values.rearrange("p t e -> p (t e)").unsqueeze(1).to_broadcast([P, PICKS, NT * NE]), ALU.mult)))
                return dve.tensor_reduce(dst, picked[:, :, :], X, ALU.add)

            after(step(take(pick_slot[:, :], slot[:, :, :])))
            dve.tensor_copy(pick_slot_u[:, :], pick_slot[:, :]).then_inc(slots_ready, 1)
            dve.wait_ge(extra_at_mm, 1)
            after(step(dve.tensor_copy(extra_at[:, :], ps[0:NE, 4, 0:1])))
            step(dve.tensor_tensor(extra_end[:, :], extra_at[:, :], extra_col[:, :], ALU.add))
            after(step(dve.tensor_scalar(ov_from[:, :], const("index", NE, NOV), extra_at[:, 0:1], None, ALU.is_ge)))
            dve.scalar_tensor_tensor(out=ov_onehot[:, :], in0=const("index", NE, NOV), scalar=extra_end[:, 0:1], in1=ov_from[:, :],
                                     op0=ALU.is_lt, op1=ALU.mult).then_inc(ov_onehot_ready, 1)
            dve.wait_ge(gates_exp, 1)
            step(dve.tensor_tensor(gg, gg, sel_g[:, :, :], ALU.mult))
            after(step(dve.tensor_tensor(ge, ge, sel_e[:, :, :], ALU.mult)))
            step(dve.tensor_reduce(top[:, 0:NT], gg, X, ALU.add))
            after(step(dve.tensor_reduce(top[:, NT:], ge, X, ALU.add)))
            after(step(dve.reciprocal(top[:, :], top[:, :])))
            step(dve.tensor_tensor(gg, gg, top[:, 0:NT].unsqueeze(2).to_broadcast([P, NT, G]), ALU.mult))
            after(step(dve.tensor_tensor(ge, ge, top[:, NT:].unsqueeze(2).to_broadcast([P, NT * G, EG]), ALU.mult)))
            dve.tensor_tensor(comb[:, :, :].rearrange("p t (g e) -> p (t g) e", g=G), ge, gate_g.unsqueeze(2).to_broadcast([P, NT * G, EG]),
                              ALU.mult).then_inc(comb_ready, 1)
            dve.wait_ge(comb_ready, 1)
            step(take(pick_w[:, :], comb[:, :, :]))
            dve.wait_ge(b2_mm, 1)
            for g in range(2):
                dve.tensor_tensor(hb[:, 2 * g:2 * g + 2, :], ps[:, 6 + g, 0:2 * D].rearrange("p (t d) -> p t d", t=2),
                                  h[:, 2 * g:2 * g + 2, :], ALU.add).then_inc(b2_added, 1)

            def rows_out(i, u):
                dve.wait_ge(rowsT_mm, i * RING + u + 1)
                dve.tensor_copy(x_rowsT[:, u % 2], ps[:, u % 2, 0:2 * P].rearrange("p (c n) -> p c n", c=2)).then_inc(rowsT_sb, 1)

            def results(i, first, last_round):
                for u in range(RING):
                    if not (last_round and u + 2 >= RING):
                        rows_out(i + (u + 2) // RING, (u + 2) % RING)
                    dve.wait_ge(down_mm, i * RING + u + 1)
                    if not first:
                        dve.wait_ge(y_dma[u], 16 * i)
                    dve.tensor_copy(y_rows[:, u, :], ps[:, 6 + u % 2, 0:D]).then_inc(y_ready, 1)

            rows_out(0, 0)
            rows_out(0, 1)
            results(0, True, False)
            with dve.Fori(1, ROUNDS - 1) as i:
                results(i, False, False)
            results(ROUNDS - 1, False, True)
            dve.wait_ge(y_dma[0], 16 * ROUNDS)
            dve.wait_ge(ov_info_ready, 2)
            tiles = dve.value_load(ov_info[0:1, NOV:NOV + 1], min_val=0, max_val=NOV)
            with dve.Fori(0, NOV) as i:
                with dve.If(tiles > i):
                    dve.wait_ge(ov_rowsT_mm, i + 1)
                    dve.tensor_copy(x_rowsT[:, 0], ps[:, 0, 0:2 * P].rearrange("p (c n) -> p c n", c=2)).then_inc(ov_rowsT_sb, 1)
                    dve.wait_ge(ov_down_mm, i + 1)
                    dve.tensor_copy(y_rows[:, 0, :], ps[:, 6, 0:D]).then_inc(ov_y_ready, 1)
                dve.nop()
            after(steps[0])
            for t in range(NT):
                dve.wait_ge(y_back_dma[t], 16 * PICKS)
                for k in range(PICKS):
                    ins = dve.scalar_tensor_tensor(out=(h if k == PICKS - 1 else hb)[:, t], in0=y_back[:, t, k],
                                                   scalar=pick_w[:, k * NT + t:k * NT + t + 1], in1=hb[:, t], op0=ALU.mult, op1=ALU.add)
                    if k == PICKS - 1:
                        ins.then_inc(h_ready, 1)
                    else:
                        after(step(ins))
            layer_norm(2)
            for t in range(NT):
                dve.wait_ge(qk_mm, NT + t + 1)
                dve.tensor_tensor(turned[:, t], ps[:, t, 0:2 * D], bqk1[:, :], ALU.add).then_inc(qk_biased, 1)
            values_out(1)
            for t in range(NT):
                x2 = turned[:, t].rearrange("p (m n r) -> p m n r", m=2, r=2)
                s2 = rope_swap[:, t, 0:2 * D].rearrange("p (m n r) -> p m n r", m=2, r=2)
                sin = const("rope_sin").rearrange("p (n r) -> p n r", r=2)
                dve.wait_ge(qk_biased, t + 1)
                for r in range(2):
                    n = step(dve.tensor_tensor(s2[:, :, :, r], x2[:, :, :, 1 - r], sin[:, :, r].unsqueeze(1).to_broadcast([P, 2, D // 2]), ALU.mult))
                after(n)
                dve.wait_ge(rope_cos_part, t + 1)
                dve.tensor_tensor(qk_pad[:, t, :, 0:HD], fexp[:, t], rope_swap[:, t, 0:2 * D].rearrange("p (h f) -> p h f", f=HD), ALU.add).then_inc(qk_pad_ready, 1)
            attention(1)
            layer_norm(3)

            dve.wait_ge(score_ready, 1)
            dve.wait_ge(ffn_dma, 16 * FFN_LOADS)
            after(step(dve.tensor_tensor(biased[:, :, :], score[:, :, :], gate_b[:, :].unsqueeze(1).to_broadcast([P, NT, E1]), ALU.add)))
            after(step(dve.tensor_reduce(group_sum[:, :, :], biased[:, :, :].rearrange("p t (g e) -> p t g e", g=G), X, ALU.add)))
            ranks(rank_g[:, :, :], group_sum[:, :, :], NT, G, "tie4")
            after(step(dve.tensor_scalar(shut[:, :, :], rank_g[:, :, :], 1.5, -BIG, ALU.is_gt, ALU.mult)))
            b3 = biased[:, :, :].rearrange("p t (g e) -> p (t g) e", g=G)
            after(step(dve.tensor_tensor(b3, b3, shut[:, :, :].rearrange("p t g -> p (t g)").unsqueeze(2).to_broadcast([P, NT * G, E1 // G]), ALU.add)))
            ranks(rank_1[:, :, :], biased[:, :, :], NT, E1, "tie8")
            after(step(dve.scalar_tensor_tensor(out=cw[:, :, :], in0=rank_1[:, :, :], scalar=1.5, in1=score[:, :, :], op0=ALU.is_lt, op1=ALU.mult)))
            after(step(dve.tensor_reduce(score_sum[:, :], cw[:, :, :], X, ALU.add)))
            after(step(dve.tensor_scalar(score_sum[:, :], score_sum[:, :], 1e-6, None, ALU.add)))
            after(step(dve.reciprocal(score_sum[:, :], score_sum[:, :])))
            after(step(dve.tensor_tensor(cw[:, :, :], cw[:, :, :], score_sum[:, :].unsqueeze(2).to_broadcast([P, NT, E1]), ALU.mult)))

            def gate_product(n, u, first=False):
                dve.wait_ge(silu_done, n + 1)
                if not first:
                    dve.wait_ge(down1_mm, n - 1)
                dve.tensor_tensor(gated[:, u, :], silu[:, u, :], ps[:, 2 * u + 1, :], ALU.mult).then_inc(gated_ready, 1)

            def add_expert(n, u):
                dve.wait_ge(down1_mm, n + 1)
                dve.wait_ge(summed, n)
                for t in range(NT):
                    ins = dve.scalar_tensor_tensor(out=h[:, t], in0=ps[:, 6 - 2 * u + t // 2, (t % 2) * D:(t % 2 + 1) * D],
                                                   scalar=cw[:, t, bass.ds(n - 1, 1)], in1=h[:, t], op0=ALU.mult, op1=ALU.add)
                ins.then_inc(summed, 1)

            gate_product(0, 0, True)
            gate_product(1, 1, True)
            dve.wait_ge(down1_mm, 1)
            dve.wait_ge(h_ready, LAST_H * NT)
            for g in range(2):
                hg = h[:, 2 * g:2 * g + 2, :]
                ins = dve.tensor_tensor(hg, ps[:, 6 + g, 0:2 * D].rearrange("p (t d) -> p t d", t=2), hg, ALU.add)
            ins.then_inc(summed, 1)
            gate_product(2, 0)
            add_expert(1, 1)
            with dve.Fori(1, N1 // 2) as i:
                gate_product(2 * i + 1, 1)
                add_expert(2 * i, 0)
                gate_product(2 * i + 2, 0)
                add_expert(2 * i + 1, 1)
            add_expert(N1 - 1, 0)


ROUNDS = NE // RING
W_LOADS = 4
ROUTE_LOADS = 4 + 4
PATCH_BANK = [3, 4, 5, 6, 7, 3]
ATTN0_LOADS = 1 + 2 + 1 + 2 + 1 + 2 + 1
ATTN1_LOADS = 6 + 2 + 2 + 2 + 1
LAST_H = 4
FFN_LOADS = 8 + 4 + 3

_INS = ['x', 'L0_tok_W', 'L0_tok_b', 'L0_attn_w_inp', 'L0_attn_b_inp', 'L0_attn_w_out', 'L0_attn_b_out', 'L0_attn_omega',
        'L0_ffn_Wg', 'L0_ffn_bg', 'L0_ffn_Wge', 'L0_ffn_bge', 'L0_ffn_W1', 'L0_ffn_b1', 'L0_ffn_W2', 'L0_ffn_b2',
        'L1_attn_Wq', 'L1_attn_bq', 'L1_attn_Wk', 'L1_attn_bk', 'L1_attn_Wv', 'L1_attn_bv', 'L1_attn_Wo', 'L1_attn_bo',
        'L1_ffn_gate_weight', 'L1_ffn_gate_bias', 'L1_ffn_w1', 'L1_ffn_w2', 'L1_ffn_w3', 'L1_ffn_sw1', 'L1_ffn_sw2', 'L1_ffn_sw3']


def kernel(**inputs):
    import concourse.bacc as bacc
    from concourse.bass_utils import run_bass_kernel_spmd

    nc = bacc.Bacc("TRN2", target_bir_lowering=False, num_devices=1)
    arrays, dram = {}, {}
    for name in _INS:
        a = np.ascontiguousarray(inputs[name])
        arrays[f"in_{name}"] = a
        dram[name] = nc.dram_tensor(f"in_{name}", a.shape, F32, kind="ExternalInput").ap()
    arrays["shape_constants"] = shape_constants()
    consts = nc.dram_tensor("shape_constants", (P, NCONST), F32, kind="ExternalInput").ap()
    out = nc.dram_tensor("out", (NIMG, SEQ, D), F32, kind="ExternalOutput").ap()
    vit_tower(nc, dram, consts, out)
    return run_bass_kernel_spmd(nc, [arrays], core_ids=[0]).results[0]["out"]
```

```python
from contextlib import ExitStack, nullcontext

import numpy as np

import concourse.bass as bass
from concourse import mybir

F32 = mybir.dt.float32
I32 = mybir.dt.int32
U32 = mybir.dt.uint32
ALU = mybir.AluOpType
ACT = mybir.ActivationFunctionType
X = mybir.AxisListType.X

P = 128
NIMG, NCH, IMG, PATCH = 8, 3, 128, 16
SIDE = IMG // PATCH
SEQ = SIDE * SIDE
TOK = NIMG * SEQ
NT = TOK // P
IPT = P // SEQ
D = 192
DA, DB = P, D - P
PD = NCH * PATCH * PATCH
KP = PD // P
H, HD = 12, 16
HPAD = 32
HG = P // HPAD
HB = H // HG
NPAIR = H // 2
VW = HD + 1
LN_EPS = 1e-5
RFM_EPS = 1e-6
G, EG = 4, 8
NE = G * EG
HID = 768
KH = HID // P
PICKS = 4
NOV = (TOK * PICKS) // P - 1
SLOTS = (NE + NOV) * P
XW = D + DB
XR = XW + 1
RING = 4
ROUNDS = NE // RING
OV_ROUNDS = -(-NOV // RING)
OVPAD = (OV_ROUNDS + 1) * RING
E1, INTER = 8, 128
N1 = E1 + 1
BIG = 1.0e30

BANK = 512

CONST = {}
_at = 0
for _name, _w in (("ident", P), ("causal", SEQ), ("future", SEQ), ("rope_cos", D), ("rope_sin", D),
                  ("before", P), ("headblock", P // HD), ("earlier", EG), ("first_slot", NE), ("ov_shift", NE),
                  ("ones", P), ("index", NOV), ("row", 1), ("pick_row", PICKS * NT), ("dump_row", 1), ("ln_eps", 1)):
    CONST[_name] = (_at, _at + _w)
    _at += _w
NCONST = _at


def shape_constants():
    c = np.zeros((P, NCONST), np.float32)

    def put(name, a):
        c[:, CONST[name][0]:CONST[name][1]] = a

    row = np.arange(P)
    pos = row % SEQ
    put("ident", np.eye(P))
    put("causal", np.arange(SEQ)[None, :] <= pos[:, None])
    put("future", -BIG * (np.arange(SEQ)[None, :] > pos[:, None]))
    half = D // 2
    freq = (1.0 / (np.float32(10000.0) ** (np.arange(half, dtype=np.float32) * np.float32(2.0) / np.float32(D)))).astype(np.float32)
    ang = pos.astype(np.float32)[:, None] * freq[None, :]
    put("rope_cos", np.repeat(np.cos(ang), 2, axis=1))
    put("rope_sin", np.stack([-np.sin(ang), np.sin(ang)], axis=2).reshape(P, D))
    put("before", row[:, None] < row[None, :])
    put("headblock", (row[:, None] // HD == np.arange(P // HD)[None, :]) * float(HD) ** -0.25)
    put("earlier", EG - np.arange(EG)[None, :])
    put("first_slot", np.arange(NE)[None, :] * P)
    put("ones", 1.0)
    put("ov_shift", (NE - 1 - np.arange(NE)[None, :]) * P)
    put("index", np.arange(NOV)[None, :])
    put("row", row[:, None])
    put("pick_row", row[:, None] + P * np.arange(PICKS * NT)[None, :])
    put("dump_row", PICKS * TOK + row[:, None])
    put("ln_eps", LN_EPS)
    return c


def vit_tower(nc, dram, consts, out, dbg=None):
    es = ExitStack()
    with es:
        def sb(name, shape, dt=F32):
            return es.enter_context(nc.sbuf_tensor(name, shape, dt))

        def sem(name):
            return es.enter_context(nc.semaphore(name))

        x_slots = nc.dram_tensor("x_slots", ((NE + OVPAD) * P, XR), F32).ap()
        y_picks = nc.dram_tensor("y_picks", (PICKS * TOK + P, D), F32).ap()

        cst = sb("cst", [P, NCONST])

        def const(name, rows=P, cols=None):
            a, b = CONST[name]
            return cst[0:rows, a:(b if cols is None else a + cols)]

        early = sb("early", [P, 2 * KP * TOK])
        x_in = early[:, 0:KP * TOK].rearrange("p (c n) -> p c n", c=NCH)
        patchesT = early[:, KP * TOK:2 * KP * TOK].rearrange("p (k n) -> p k n", k=KP)
        w13_raw = early[:, 0:2 * N1 * P].rearrange("p (e m d) -> p e m d", e=N1, m=2)
        w13_raw_tail = early[:, 2 * N1 * P:3 * N1 * P].rearrange("p (e c) -> p e c", e=N1)
        w2_place = early[:, 3 * N1 * P:5 * N1 * P].rearrange("p (e c) -> p e c", e=N1)
        w2_raw, w2_raw_tail = w2_place[:, :, 0:P], w2_place[0:DB, :, P:2 * P]
        w13T, w13T_tail, w2T = w13_raw, w13_raw_tail, w2_place[:, :, 0:D]

        wtok = sb("wtok", [P, 2, PD])
        wtokT = sb("wtokT", [P, KP, D])
        btok = sb("btok", [P, D])
        h = sb("h", [P, NT, D])
        hb = sb("hb", [P, NT, D])
        stats = sb("stats", [P, NT, 6])
        mv = sb("mv", [P, NT, 2])
        rstd = sb("rstd", [P, NT, 1])
        xn = sb("xn", [P, NT, XR])
        xnT = sb("xnT", [P, 2, TOK])

        wqkv0 = sb("wqkv0", [P, 2, 3 * D])
        bqk0 = sb("bqk0", [P, 3])
        bv = [sb(f"bv{a}", [P, D // 2]) for a in range(2)]
        wo = [sb(f"wo{a}", [P, 2, D]) for a in range(2)]
        bo = [sb(f"bo{a}", [P, D]) for a in range(2)]
        omega8 = sb("omega8", [HD, P // HD, HD])
        omega_bd = sb("omega_bd", [P, P])
        wqkv1 = sb("wqkv1", [P, 2, 3 * D])
        bqk1 = sb("bqk1", [P, 2 * D])

        qkT0 = sb("qkT0", [P, 3, TOK])
        qk_pad = sb("qk_pad", [P, NT, 2 * H, HPAD])
        qk_padT = sb("qk_padT", [P, NT, 2 * HB, P])
        fsum = sb("fsum", [P, NT, 2 * H])
        foff = sb("foff", [P, NT, 2 * H])
        fmax = sb("fmax", [P, NT, 1])
        fexp = sb("fexp", [P, NT, 2 * H, HD])
        turned = sb("turned", [P, NT, 2 * D])
        probs = sb("probs", [P, NT, H, SEQ])
        probsT = sb("probsT", [P, NT, NPAIR, P])
        x_by_col = probsT[:, :, :, :].rearrange("p t j n -> p (t j n)").rearrange("p (c w n) -> p c w n", c=NCH, w=SIDE)
        rowmax = sb("rowmax", [P, NT, H])
        v_bd = sb("v_bd", [P, NIMG, NPAIR, 2 * VW])
        rden = sb("rden", [P, NT, H])
        att = sb("att", [P, NT, XW])
        attT = sb("attT", [P, NT, 2, P])

        wroute = sb("wroute", [P, 2, G + NE])
        broute = sb("broute", [P, G + NE])
        b1_rows, b2_rows = sb("b1_rows", [NE, HID]), sb("b2_rows", [NE, D])
        b1T = sb("b1T", [P, KH, NE + OVPAD])
        ggl, gel = sb("ggl", [P, NT, G]), sb("gel", [P, NT * G, EG])
        work_g, work_e = sb("work_g", [P, NT, G]), sb("work_e", [P, NT * G, EG])
        rest_g, rest_e = sb("rest_g", [P, NT, G]), sb("rest_e", [P, NT * G, EG])
        best = sb("best", [P, 2, NT * (1 + G)])
        first_of = sb("first_of", [P, NT * (1 + G)])
        sel_g, sel_e = sb("sel_g", [P, NT, G]), sb("sel_e", [P, NT * G, EG])
        chosen = sb("chosen", [P, NT, NE])
        gates = sb("gates", [P, 2, NT * (1 + G)])
        gate_sum = sb("gate_sum", [P, NT * (1 + G)])
        group_gate = sb("group_gate", [P, 2, NT, G])
        comb = sb("comb", [P, NT, NE])
        combT = sb("combT", [NE, TOK])
        extra = sb("extra", [P, 1 + NE])
        extra_sum = sb("extra_sum", [P, 1 + NE])
        shift = sb("shift", [P, NE])
        home = sb("home", [P, NT, NE])
        slot = sb("slot", [P, NT, NE])
        extra_col, extra_at, extra_end = sb("extra_col", [NE, 1]), sb("extra_at", [NE, 1]), sb("extra_end", [NE, 1])
        ov_from, ov_onehot = sb("ov_from", [NE, NOV]), sb("ov_onehot", [NE, NOV])
        tile_expert, ov_tiles = sb("tile_expert", [1, OVPAD], I32), sb("ov_tiles", [1, 1], I32)
        pick_g, pick_e = sb("pick_g", [P, 2, NT, G]), sb("pick_e", [P, 2, NT, NE])
        pick = sb("pick", [P, PICKS, NT, NE])
        picked = sb("picked", [P, PICKS * NT, NE])
        pick_slot, pick_w = sb("pick_slot", [P, PICKS * NT]), sb("pick_w", [P, PICKS * NT])
        pick_slot_u = sb("pick_slot_u", [P, PICKS * NT], U32)
        empty_row = sb("empty_row", [P, XR])
        w1 = sb("w1", [P, RING, HID])
        w1_tail = sb("w1_tail", [P, RING, HID // 2])
        w2 = sb("w2", [P, RING, KH, D])
        x_rows = qkT0[:, :, :].rearrange("p c n -> p (c n)")[:, 0:RING * XR].rearrange("p (u n) -> p u n", u=RING)
        after_exp = fexp[:, :, :, :].rearrange("p t h f -> p (t h f)")
        x_rowsT = after_exp[:, 0:4 * P].rearrange("p (b c n) -> p b c n", b=2, c=2)
        y_rows = after_exp[:, 4 * P:4 * P + RING * D].rearrange("p (u n) -> p u n", u=RING)
        hidden = turned[:, :, :].rearrange("p t n -> p (t n)").rearrange("p (b c n) -> p b c n", b=2, c=KH)
        y_row = sb("y_row", [P, RING], U32)
        after_probs = probs[:, :, :, :].rearrange("p t h k -> p (t h k)")
        xn_of_pick = [xn[:, :, :], wtok[:, :, :].rearrange("p c n -> p (c n)")[:, 0:NT * XR].rearrange("p (t n) -> p t n", t=NT)]
        xn_of_pick += [after_probs[:, n * NT * XR:(n + 1) * NT * XR].rearrange("p (t n) -> p t n", t=NT) for n in range(PICKS - 2)]
        y_back = qk_padT[:, :, :, :].rearrange("p t j n -> p t (j n)").rearrange("p t (k d) -> p t k d", k=PICKS)

        gate_rows, gate_wT, gate_b = empty_row[0:E1, 0:XW], sb("gate_wT", [P, 2, E1]), sb("gate_b", [P, E1])
        score, biased = sb("score", [P, NT, E1]), sb("biased", [P, NT, E1])
        group_sum, shut = sb("group_sum", [P, NT, G]), sb("shut", [P, NT, G])
        chosen_1 = [pick_e[:, r, 0, :].rearrange("p (t e) -> p t e", t=NT) for r in range(2)]
        score_sum, cw = sb("score_sum", [P, NT]), sb("cw", [P, NT, E1])
        rope_swap = after_probs.rearrange("p (t n) -> p t n", t=NT)
        silu = after_probs[:, 0:2 * TOK].rearrange("p (b n) -> p b n", b=2)
        gated = after_probs[:, 2 * TOK:4 * TOK].rearrange("p (b n) -> p b n", b=2)

        ps = es.enter_context(nc.psum_tensor("ps", [P, 8, BANK], F32))

        x_in_dma = [sem(f"x_in_dma{c}") for c in range(NCH)]
        wtok_dma, ident_dma, const_dma, attn0_dma, attn1_dma = sem("wtok_dma"), sem("ident_dma"), sem("const_dma"), sem("attn0_dma"), sem("attn1_dma")
        pads_zeroed = sem("pads_zeroed")
        x_by_col_ready = [sem(f"x_by_col_ready{c}") for c in range(NCH)]
        wtokT_mm, wtokT_sb = sem("wtokT_mm"), sem("wtokT_sb")
        patches_mm, patches_act, patches_dve = sem("patches_mm"), sem("patches_act"), sem("patches_dve")
        embed_mm = sem("embed_mm")
        h_ready, hb_ready = sem("h_ready"), sem("hb_ready")
        moments, deviation = sem("moments"), sem("deviation")
        xn_ready, xnT_mm, xnT_sb = sem("xn_ready"), sem("xnT_mm"), sem("xnT_sb")
        omega_mm, omega_sb = sem("omega_mm"), sem("omega_sb")
        qkT0_mm, qkT0_sb = sem("qkT0_mm"), sem("qkT0_sb")
        v_mm, v_sb = sem("v_mm"), sem("v_sb")
        qk_mm, feat_centred, feat_exp, qk_pad_ready = sem("qk_mm"), sem("feat_centred"), sem("feat_exp"), sem("qk_pad_ready")
        rope_sum = sem("rope_sum")
        qk_padT_mm, qk_padT_sb = sem("qk_padT_mm"), sem("qk_padT_sb")
        scores_mm, scores_read, centred, probs_exp = sem("scores_mm"), sem("scores_read"), sem("centred"), sem("probs_exp")
        probsT_mm, probsT_sb = sem("probsT_mm"), sem("probsT_sb")
        att_mm, att_ready, attT_mm, attT_sb, proj_mm = sem("att_mm"), sem("att_ready"), sem("attT_mm"), sem("attT_sb"), sem("proj_mm")
        route_dma, empty_dma, empty_ready = sem("route_dma"), sem("empty_dma"), sem("empty_ready")
        logits_mm, chosen_ready, counts_mm, count_col_mm = sem("logits_mm"), sem("chosen_ready"), sem("counts_mm"), sem("count_col_mm")
        ids_written, xn_copied, y_row_ready = sem("ids_written"), sem("xn_copied"), sem("y_row_ready")
        pool_may = sem("pool_may")
        gates_centred, gates_exp, comb_ready = sem("gates_centred"), sem("gates_exp"), sem("comb_ready")
        extra_col_ready, extra_at_mm, ov_onehot_ready, ov_mm, tile_info_ready = (
            sem("extra_col_ready"), sem("extra_at_mm"), sem("ov_onehot_ready"), sem("ov_mm"), sem("tile_info_ready"))
        b1T_sb, slots_ready, scatter_dma = sem("b1T_sb"), sem("slots_ready"), sem("scatter_dma")
        combT_mm, combT_sb, b2_mm, b2_added = sem("combT_mm"), sem("combT_sb"), sem("b2_mm"), sem("b2_added")
        w_dma, x_dma, y_dma = ([sem(f"{n}{u}") for u in range(RING)] for n in ("w_dma", "x_dma", "y_dma"))
        rowsT_mm, rowsT_sb, up_mm, gelu_done, down_mm, y_ready = (
            sem("rowsT_mm"), sem("rowsT_sb"), sem("up_mm"), sem("gelu_done"), sem("down_mm"), sem("y_ready"))
        y_back_dma = [sem(f"y_back_dma{t}") for t in range(NT)]
        ffn_dma, ffn_wT_mm, ffn_w13T_sb, ffn_w2T_sb = sem("ffn_dma"), sem("ffn_wT_mm"), sem("ffn_w13T_sb"), sem("ffn_w2T_sb")
        qk_biased, rope_cos_part = sem("qk_biased"), sem("rope_cos_part")
        gate_mm, score_ready = sem("gate_mm"), sem("score_ready")
        up1_mm, silu_done, gated_ready, down1_mm, summed = sem("up1_mm"), sem("silu_done"), sem("gated_ready"), sem("down1_mm"), sem("summed")
        dve_step = sem("dve_step")
        out_dma = sem("out_dma")

        ident = const("ident")

        def number_of_ov_tiles(engine):
            engine.wait_ge(tile_info_ready, TILE_INFO)
            return engine.value_load(ov_tiles[0:1, 0:1], min_val=0, max_val=NOV)

        def where_tile(engine, tiles, ov_round, step):
            if ov_round is None or (isinstance(ov_round, int) and ov_round * RING + step < 0):
                return nullcontext()
            return engine.If(tiles > ov_round * RING + step)

        def rounds(engine, tiles, body):
            body(0, None, True)
            with engine.Fori(1, ROUNDS - 1) as i:
                body(i, None, False)
            body(ROUNDS - 1, -1, False)
            with engine.Fori(0, OV_ROUNDS) as r:
                with engine.If(tiles > r * RING):
                    body(r + ROUNDS, r, False)
                engine.nop()
        NATTN = 8

        def load_columns(q, dst, src, done):
            q.dma_start(dst[:, 0, :], src[0:DA, :]).then_inc(done, 16)
            q.dma_start(dst[0:DB, 1, :], src[DA:D, :]).then_inc(done, 16)

        def load_bv(q, dst, src, done):
            s = src.rearrange("(j p d) -> p j d", p=2, d=HD)
            for par in range(2):
                q.dma_start(dst[par * SEQ:(par + 1) * SEQ, :].rearrange("p (j d) -> p j d", d=HD),
                            s[par:par + 1].to_broadcast([SEQ, NPAIR, HD])).then_inc(done, 16)

        def load_row(q, dst, src, done):
            q.dma_start(dst[:, :], src.unsqueeze(0).to_broadcast([P, src.shape[0]])).then_inc(done, 16)

        def patch_job(copy, n):
            c, part = n // 2, n % 2
            dst = patchesT[:, 2 * c:2 * c + 2, :].rearrange("p k (s w) -> p k s w", w=SIDE)[:, :, :, part * 4:part * 4 + 4]
            src = ps[:, PATCH_BANK[n], :].rearrange("p (w k s) -> p k s w", w=4, k=2)
            return copy(dst, src)

        def regroup_channel(copy, c):
            return copy(x_by_col[:, c].rearrange("p w (r q) -> p w r q", q=PATCH),
                        x_in[:, c, :].rearrange("p (r w q) -> p w r q", w=SIDE, q=PATCH))

        block = es.enter_context(nc.Block())

        @block.sync
        def _(sp):
            xv = dram["x"].rearrange("b c (hp hh r) w -> c hh b hp (r w)", hp=SIDE, hh=2)
            for c in range(NCH):
                for hh in range(2):
                    sp.dma_start(x_in[hh * SEQ:(hh + 1) * SEQ, c, :], xv[c, hh]).then_inc(x_in_dma[c], 16)
            sp.dma_start(cst[:, P:NCONST], consts[:, P:NCONST]).then_inc(const_dma, 16)
            load_row(sp, btok[:, :], dram["L0_tok_b"], attn0_dma)
            load_columns(sp, wqkv0, dram["L0_attn_w_inp"][0], attn0_dma)
            sp.dma_start(bqk0[:, :], dram["L0_attn_b_inp"][0:2 * D].rearrange("(c p) -> p c", p=P), allow_slow_non_contiguous=True).then_inc(attn0_dma, 16)
            load_bv(sp, bv[0], dram["L0_attn_b_inp"][2 * D:3 * D], attn0_dma)
            sp.dma_start(omega8[:, :, :], dram["L0_attn_omega"].unsqueeze(1).to_broadcast([HD, P // HD, HD])).then_inc(attn0_dma, 16)
            load_columns(sp, wo[0], dram["L0_attn_w_out"][0], attn0_dma)
            load_row(sp, bo[0], dram["L0_attn_b_out"], attn0_dma)
            w1v = wqkv1[:, :, :]
            for n, name in enumerate(("L1_attn_Wq", "L1_attn_Wk", "L1_attn_Wv")):
                load_columns(sp, w1v[:, :, n * D:(n + 1) * D], dram[name], attn1_dma)
            load_row(sp, bqk1[:, 0:D], dram["L1_attn_bq"], attn1_dma)
            load_row(sp, bqk1[:, D:2 * D], dram["L1_attn_bk"], attn1_dma)
            load_bv(sp, bv[1], dram["L1_attn_bv"], attn1_dma)
            load_columns(sp, wo[1], dram["L1_attn_Wo"], attn1_dma)
            load_row(sp, bo[1], dram["L1_attn_bo"], attn1_dma)

            pw = dram["L0_ffn_Wge"].rearrange("g d e -> d g e")
            for c, (a, b) in enumerate(((0, DA), (DA, D))):
                sp.dma_start(wroute[0:b - a, c, 0:G], dram["L0_ffn_Wg"][a:b, :]).then_inc(route_dma, 16)
                sp.dma_start(wroute[0:b - a, c, G:G + NE].rearrange("p (g e) -> p g e", g=G), pw[a:b]).then_inc(route_dma, 16)
            sp.dma_start(broute[:, 0:G], dram["L0_ffn_bg"].unsqueeze(0).to_broadcast([P, G])).then_inc(route_dma, 16)
            sp.dma_start(broute[:, G:G + NE], dram["L0_ffn_bge"].rearrange("g e -> (g e)").unsqueeze(0).to_broadcast([P, NE])).then_inc(route_dma, 16)
            sp.dma_start(b1_rows[:, :], dram["L0_ffn_b1"]).then_inc(route_dma, 16)
            sp.dma_start(b2_rows[:, :], dram["L0_ffn_b2"]).then_inc(route_dma, 16)
            sp.wait_ge(empty_ready, 2)
            sp.dma_start(x_slots[0:SLOTS, :].rearrange("(r p) c -> p r c", p=P), empty_row[:, :].unsqueeze(1).to_broadcast([P, SLOTS // P, XR])).then_inc(empty_dma, 16)

            def load_expert(e, u, done):
                one = bass.ds(e, 1)
                w1d = dram["L0_ffn_W1"][one, :, :].rearrange("a d m -> (a d) m")
                sp.dma_start(w1[:, u, :], w1d[0:DA, :]).then_inc(done, 16)
                sp.dma_start(w1_tail[0:DB, u, :], w1d[DA:D, 0:HID // 2]).then_inc(done, 16)
                sp.dma_start(w1_tail[DB:P, u, :], w1d[DA:D, HID // 2:HID]).then_inc(done, 16)
                sp.dma_start(w2[:, u], dram["L0_ffn_W2"][one, :, :].rearrange("a (c p) d -> p (a c) d", p=P)).then_inc(done, 16)

            def load_rows(tile, u, done):
                sp.dma_start(x_rows[:, u, :], x_slots[bass.ds(tile * P, P), :]).then_inc(done, 16)

            for u in range(RING):
                load_expert(u, u, w_dma[u])
            sp.wait_ge(embed_mm, NT)
            for m, (name, shared) in enumerate((("L1_ffn_w1", "L1_ffn_sw1"), ("L1_ffn_w3", "L1_ffn_sw3"))):
                tail = slice(m * DB, (m + 1) * DB)
                sp.dma_start(w13_raw[:, 0, m, :], dram[shared][:, 0:DA]).then_inc(ffn_dma, 16)
                sp.dma_start(w13_raw_tail[:, 0, tail], dram[shared][:, DA:D]).then_inc(ffn_dma, 16)
                w = dram[name].rearrange("e i d -> i e d")
                sp.dma_start(w13_raw[:, 1:N1, m, :], w[:, :, 0:DA]).then_inc(ffn_dma, 16)
                sp.dma_start(w13_raw_tail[:, 1:N1, tail], w[:, :, DA:D]).then_inc(ffn_dma, 16)
            sp.dma_start(w2_raw[:, 0, :], dram["L1_ffn_sw2"][0:DA, :]).then_inc(ffn_dma, 16)
            sp.dma_start(w2_raw_tail[:, 0, :], dram["L1_ffn_sw2"][DA:D, :]).then_inc(ffn_dma, 16)
            w = dram["L1_ffn_w2"].rearrange("e d i -> d e i")
            sp.dma_start(w2_raw[:, 1:N1, :], w[0:DA]).then_inc(ffn_dma, 16)
            sp.dma_start(w2_raw_tail[:, 1:N1, :], w[DA:D]).then_inc(ffn_dma, 16)
            sp.wait_ge(empty_dma, 16)
            sp.dma_start(gate_rows[:, 0:D], dram["L1_ffn_gate_weight"]).then_inc(ffn_dma, 16)
            sp.dma_start(gate_rows[:, D:XW], dram["L1_ffn_gate_weight"][:, DA:D]).then_inc(ffn_dma, 16)
            load_row(sp, gate_b, dram["L1_ffn_gate_bias"], ffn_dma)
            sp.wait_ge(scatter_dma, 16 * PICKS * NT)
            for u in range(RING):
                load_rows(u, u, x_dma[u])

            tiles = number_of_ov_tiles(sp)

            def feed(i, ov_round, first):
                for u in range(RING):
                    with where_tile(sp, tiles, ov_round, u):
                        with where_tile(sp, tiles, ov_round, u + RING):
                            sp.wait_ge(down_mm, i * RING + u + 1)
                            tile = (i + 1) * RING + u
                            if ov_round is None:
                                e = tile
                            else:
                                e = sp.value_load(tile_expert[0:1, bass.ds((ov_round + 1) * RING + u, 1)], min_val=0, max_val=NE - 1)
                            load_expert(e, u, w_dma[u])
                            sp.wait_ge(y_row_ready, i * RING + u + 1)
                            load_rows(tile, u, x_dma[u])

            rounds(sp, tiles, feed)
            for u in range(RING):
                sp.wait_ge(y_dma[u], 16 * ((tiles + (NE + RING - 1 - u)) // RING))
            y_tok = y_picks[0:PICKS * TOK, :].rearrange("(k t p) d -> t p k d", k=PICKS, p=P)
            for t in range(NT):
                sp.dma_start(y_back[:, t], y_tok[t]).then_inc(y_back_dma[t], 16)

            sp.wait_ge(summed, N1)
            sp.dma_start(out.rearrange("(t i) s d -> (i s) t d", t=NT), h[:, :, :]).then_inc(out_dma, 16)
            sp.wait_ge(out_dma, 16)

        @block.gpsimd
        def _(pool):
            pool.memset(empty_row[:, :], 0.0).then_inc(empty_ready, 1)
            pool.wait_ge(empty_ready, 1)
            pool.wait_ge(const_dma, 16)
            pool.tensor_copy(empty_row[:, XW:XR].bitcast(U32), const("dump_row")).then_inc(empty_ready, 1)
            pool.memset(qk_pad[:, :, :, HD:HPAD], 0.0).then_inc(pads_zeroed, 1)
            pool.memset(v_bd[:, :, :, :], 0.0).then_inc(pads_zeroed, 1)
            pool.memset(att[:, :, D:XW], 0.0).then_inc(pads_zeroed, 1)
            pool.wait_ge(pads_zeroed, 3)
            for par in range(2):
                pool.memset(v_bd[par * SEQ:(par + 1) * SEQ, :, :, par * VW + HD:par * VW + HD + 1], 1.0).then_inc(pads_zeroed, 1)
            pool.wait_ge(pads_zeroed, 5)
            pool.wait_ge(attn0_dma, 16 * ATTN0_LOADS)
            for a in range(2):
                if a == 1:
                    pool.wait_ge(attn1_dma, 16 * ATTN1_LOADS)
                    h_round = 2
                else:
                    h_round = 0
                for t in range(NT):
                    pool.wait_ge(h_ready, h_round * NT + t + 1)
                    pool.tensor_tensor(hb[:, t], h[:, t], bo[a][:, :], ALU.add).then_inc(hb_ready, 1)
                if a == 0:
                    for t in range(NT):
                        pool.wait_ge(feat_exp, t + 1)
                        pool.tensor_scalar(qk_pad[:, t, :, 0:HD], fexp[:, t], RFM_EPS, 1.0, ALU.add, ALU.mult).then_inc(qk_pad_ready, 1)
                    pool.wait_ge(xn_ready, 2 * NT)
                    for k in range(PICKS):
                        pool.tensor_copy(xn_of_pick[k][:, :, XW:XR].bitcast(U32), const("pick_row")[:, k * NT:(k + 1) * NT].unsqueeze(2)).then_inc(ids_written, 1)
                    pool.wait_ge(ids_written, PICKS)
                    pool.wait_ge(empty_dma, 16)
                    pool.wait_ge(slots_ready, 1)
                    for k in range(PICKS):
                        if k >= 1:
                            pool.wait_ge(xn_copied, k)
                        for t in range(NT):
                            pool.indirect_dma_start(out=x_slots[0:SLOTS, :], out_offset=bass.IndirectOffsetOnAxis(ap=pick_slot_u[:, k * NT + t:k * NT + t + 1], axis=0),
                                                    in_=xn_of_pick[k][:, t, :], in_offset=None).then_inc(scatter_dma, 16)
                    tiles = number_of_ov_tiles(pool)

                    def send(i, ov_round, first):
                        for u in range(RING):
                            with where_tile(pool, tiles, ov_round, u):
                                pool.wait_ge(x_dma[u], 16 * (i + 1))
                                if not (first and u == 0):
                                    pool.wait_ge(y_dma[(u - 1) % RING], 16 * (i + 1 if u else i))
                                pool.sem_inc(pool_may, 1)
                                pool.tensor_copy(y_row[:, u:u + 1], x_rows[:, u, XW:XR].bitcast(U32)).then_inc(y_row_ready, 1)
                                pool.wait_ge(y_row_ready, i * RING + u + 1)
                                pool.wait_ge(y_ready, i * RING + u + 1)
                                pool.sem_inc(pool_may, 1)
                                pool.indirect_dma_start(out=y_picks, out_offset=bass.IndirectOffsetOnAxis(ap=y_row[:, u:u + 1], axis=0),
                                                        in_=y_rows[:, u, :], in_offset=None).then_inc(y_dma[u], 16)

                    rounds(pool, tiles, send)
                else:
                    for t in range(NT):
                        pool.wait_ge(qk_biased, t + 1)
                        pool.tensor_tensor(fexp[:, t].rearrange("p h f -> p (h f)").rearrange("p (m n) -> p m n", m=2),
                                           turned[:, t].rearrange("p (m n) -> p m n", m=2),
                                           const("rope_cos").unsqueeze(1).to_broadcast([P, 2, D]), ALU.mult).then_inc(rope_cos_part, 1)

        @block.scalar
        def _(act):
            act.dma_start(ident, consts[:, 0:P]).then_inc(ident_dma, 16)
            act.dma_start(wtok[:, 0, :], dram["L0_tok_W"][0:DA, :]).then_inc(wtok_dma, 16)
            act.dma_start(wtok[0:DB, 1, :], dram["L0_tok_W"][DA:D, :]).then_inc(wtok_dma, 16)

            def turned_tokens(r):
                act.wait_ge(moments, (r + 1) * NT)
                act.activation(rstd[:, :, 0], mv[:, :, 1], ACT.Sqrt, bias=const("ln_eps")).then_inc(deviation, 1)
                for t in range(NT):
                    act.wait_ge(xnT_mm, r * NT + t + 1)
                    act.copy(xnT[:, :, t * P:(t + 1) * P], ps[:, 2 * t + 1, 0:2 * P].rearrange("p (c n) -> p c n", c=2)).then_inc(xnT_sb, 1)

            act.wait_ge(x_in_dma[1], 32)
            regroup_channel(act.copy, 1).then_inc(x_by_col_ready[1], 1)
            for n in range(0, 2 * NCH, 2):
                act.wait_ge(patches_mm, n + 1)
                patch_job(act.copy, n).then_inc(patches_act, 1)
            turned_tokens(0)
            act.wait_ge(attn0_dma, 16 * ATTN0_LOADS)
            for c in range(3):
                act.wait_ge(qkT0_mm, c + 1)
                act.activation(qkT0[:, c, :], ps[:, c, :], ACT.Identity, bias=bqk0[:, c:c + 1]).then_inc(qkT0_sb, 1)
            for t in range(NT):
                act.wait_ge(feat_centred, t + 1)
                act.activation(fexp[:, t].rearrange("p h f -> p (h f)"), turned[:, t], ACT.Exp).then_inc(feat_exp, 1)

            def attention(a):
                for t in range(NT):
                    act.wait_ge(qk_padT_mm, NT * a + t + 1)
                    bank = TURN_BANK[a][t]
                    act.copy(qk_padT[:, t].rearrange("p (b j) n -> p b (j n)", b=2), ps[:, bank:bank + 2, 0:HB * P]).then_inc(qk_padT_sb, 1)
                if a == 1:
                    for t in range(NT):
                        act.wait_ge(centred, t + 1)
                        act.activation(probs[:, t].rearrange("p h k -> p (h k)"), probs[:, t].rearrange("p h k -> p (h k)"),
                                       ACT.Exp, scale=float(HD) ** -0.5).then_inc(probs_exp, 1)
                for t in range(NT):
                    act.wait_ge(probsT_mm, NT * a + t + 1)
                    act.copy(probsT[:, t].rearrange("p (b j) n -> p b (j n)", b=2), ps[:, 2 * t:2 * t + 2, 0:NPAIR // 2 * P]).then_inc(probsT_sb, 1)
                for t in range(NT):
                    act.wait_ge(attT_mm, NT * a + t + 1)
                    act.copy(attT[:, t], ps[:, 2 * t + 1, 0:2 * P].rearrange("p (c n) -> p c n", c=2)).then_inc(attT_sb, 1)

            attention(0)
            turned_tokens(1)
            for k in range(1, PICKS):
                act.copy(xn_of_pick[k][:, :, 0:XW], xn[:, :, 0:XW]).then_inc(xn_copied, 1)
            act.wait_ge(gates_centred, 1)
            act.activation(gates[:, 1, :], gates[:, 1, :], ACT.Exp).then_inc(gates_exp, 1)
            act.wait_ge(ov_mm, 1)
            act.copy(b1T[:, :, 0:NE], ps[:, 5, 0:KH * NE].rearrange("p (c e) -> p c e", c=KH)).then_inc(b1T_sb, 1)
            act.copy(b1T[:, :, NE:NE + NOV], ps[:, 5, 256:256 + KH * NOV].rearrange("p (c e) -> p c e", c=KH)).then_inc(b1T_sb, 1)
            act.copy(tile_expert[0:1, 0:NOV], ps[0:1, 5, 384:384 + NOV]).then_inc(tile_info_ready, 1)
            act.wait_ge(combT_mm, 1)
            act.copy(combT[:, :], ps[0:NE, 1, 0:TOK]).then_inc(combT_sb, 1)
            act.wait_ge(b1T_sb, 2)
            for e in range(N1):
                act.wait_ge(ffn_wT_mm, e + 1)
                bank = 2 * (e % 4)
                act.copy(w13T[:, e].rearrange("p m i -> p (m i)"), ps[:, bank, 0:2 * P]).then_inc(ffn_w13T_sb, 1)
                act.copy(w13T_tail[:, e], ps[:, bank, 2 * P:3 * P]).then_inc(ffn_w13T_sb, 1)
            act.wait_ge(ffn_wT_mm, N1 + 1)
            act.copy(gate_wT[:, :, :].rearrange("p c e -> p (c e)"), ps[:, 2, 0:2 * E1]).then_inc(ffn_w13T_sb, 1)

            tiles = number_of_ov_tiles(act)

            def gelus(i, ov_round, first):
                for u in range(RING):
                    tile = i * RING + u
                    with where_tile(act, tiles, ov_round, u):
                        act.wait_ge(up_mm, tile + 1)
                        for c in range(KH):
                            last = act.activation(hidden[:, u % 2, c, :], ps[:, 2 + 2 * (u % 2) + c // 3, (c % 3) * P:(c % 3 + 1) * P], ACT.Gelu,
                                                  bias=b1T[:, c, bass.ds(tile, 1)])
                        last.then_inc(gelu_done, 1)

            rounds(act, tiles, gelus)
            turned_tokens(2)
            attention(1)
            turned_tokens(3)
            act.wait_ge(gate_mm, 1)
            act.activation(score[:, :, :].rearrange("p t e -> p (t e)"), ps[:, 4, 0:NT * E1], ACT.Sigmoid).then_inc(score_ready, 1)

            def silus(n, u, first=False):
                act.wait_ge(up1_mm, n + 1)
                if not first:
                    act.wait_ge(gated_ready, n - 1)
                act.activation(silu[:, u, :], ps[:, 2 * u, :], ACT.Silu).then_inc(silu_done, 1)

            silus(0, 0, True)
            silus(1, 1, True)
            silus(2, 0)
            with act.Fori(1, N1 // 2) as i:
                silus(2 * i + 1, 1)
                silus(2 * i + 2, 0)

        @block.tensor
        def _(pe):
            pe.wait_ge(ident_dma, 16)
            pe.wait_ge(wtok_dma, 32)
            for k in range(KP):
                o = (k % 2) * D
                nc.tensor.transpose(ps[:, k // 2, o:o + DA], wtok[:, 0, k * P:(k + 1) * P], ident)
                nc.tensor.transpose(ps[:, k // 2, o + DA:o + D], wtok[0:DB, 1, k * P:(k + 1) * P], ident[0:DB, 0:DB]).then_inc(wtokT_mm, 1)
            for n in range(2 * NCH):
                c, part = n // 2, n % 2
                if part == 0:
                    pe.wait_ge(x_by_col_ready[c], 1)
                if n == 5:
                    pe.wait_ge(patches_act, 1)
                for w in range(4):
                    last = nc.tensor.transpose(ps[:, PATCH_BANK[n], w * P:(w + 1) * P], x_by_col[:, c, part * 4 + w], ident)
                last.then_inc(patches_mm, 1)
            pe.wait_ge(wtokT_sb, KP // 2)
            pe.wait_ge(patches_act, NCH)
            pe.wait_ge(patches_dve, NCH)
            for t in range(NT):
                if t == 3:
                    pe.wait_ge(h_ready, 1)
                for k in range(KP):
                    last = nc.tensor.matmul(ps[:, t % 3, 0:D], patchesT[:, k, t * P:(t + 1) * P], wtokT[:, k, :],
                                            start=(k == 0), stop=(k == KP - 1))
                last.then_inc(embed_mm, 1)

            def turn_tokens(r):
                for t in range(NT):
                    pe.wait_ge(xn_ready, r * NT + t + 1)
                    for c in range(2):
                        last = nc.tensor.transpose(ps[:, 2 * t + 1, c * P:(c + 1) * P], xn[:, t, c * P:(c + 1) * P], ident)
                    last.then_inc(xnT_mm, 1)

            def values(wv):
                w = wv.rearrange("p c (j q d) -> p c q j d", q=2, d=HD)
                for b in range(NIMG):
                    for q in range(2):
                        dst = ps[q * SEQ:(q + 1) * SEQ, 6 + b // 4, (b % 4) * (D // 2):(b % 4 + 1) * (D // 2)]
                        for c, rows in ((0, DA), (1, DB)):
                            last = nc.tensor.matmul(dst, xnT[0:rows, c, b * SEQ:(b + 1) * SEQ], w[0:rows, c, q],
                                                    start=(c == 0), stop=(c == 1))
                    if b % 4 == 3:
                        last.then_inc(v_mm, 1)

            def attention(a):
                for t in range(NT):
                    pe.wait_ge(qk_pad_ready, NT * a + t + 1)
                    if a == 0 and t == 1:
                        pe.wait_ge(v_sb, 4)
                    if TURN_BANK[a][t] in TURN_BANK[a][:t]:
                        pe.wait_ge(qk_padT_sb, NT * a + TURN_BANK[a].index(TURN_BANK[a][t]) + 1)
                    if a == 1 and t == 2:
                        pe.wait_ge(qk_biased, NT)
                    for j in range(2 * HB):
                        last = nc.tensor.transpose(ps[:, TURN_BANK[a][t] + j // HB, (j % HB) * P:(j % HB + 1) * P],
                                                   qk_pad[:, t].rearrange("p h f -> p (h f)")[:, j * P:(j + 1) * P], ident)
                    last.then_inc(qk_padT_mm, 1)
                for t in range(NT):
                    if t == 0:
                        pe.wait_ge(qk_padT_sb, NT * a + (3 if a else 1))
                    if t == 1:
                        pe.wait_ge(qk_padT_sb, NT * a + NT)
                        pe.wait_ge(v_sb, 4 * (a + 1))
                    if t >= 2:
                        pe.wait_ge(scores_read, NT * a + t - 1)
                    for i in range(HG):
                        for j in range(HB):
                            for b in range(IPT):
                                rows, cols = slice(i * HPAD, i * HPAD + HD), slice(b * SEQ, (b + 1) * SEQ)
                                last = nc.tensor.matmul(ps[b * SEQ:(b + 1) * SEQ, 4 * (t % 2) + i, j * SEQ:(j + 1) * SEQ],
                                                        qk_padT[rows, t, j, cols], qk_padT[rows, t, HB + j, cols], start=True, stop=True)
                    last.then_inc(scores_mm, 1)
                for t in range(NT):
                    pe.wait_ge(scores_read, NT * a + (3 if t < 2 else 4))
                    if a == 1:
                        pe.wait_ge(probs_exp, t + 1)
                    for j in range(NPAIR):
                        last = nc.tensor.transpose(ps[:, 2 * t + j // 3, (j % 3) * P:(j % 3 + 1) * P],
                                                   probs[:, t, 2 * j:2 * j + 2, :].rearrange("p h k -> p (h k)"), ident)
                    last.then_inc(probsT_mm, 1)
                pe.wait_ge(v_sb, 4 * (a + 1))
                for t in range(NT):
                    pe.wait_ge(probsT_sb, NT * a + t + 1)
                    for b in range(IPT):
                        for j in range(NPAIR):
                            last = nc.tensor.matmul(ps[b * SEQ:(b + 1) * SEQ, 2 * t, j * 2 * VW:(j + 1) * 2 * VW],
                                                    probsT[:, t, j, b * SEQ:(b + 1) * SEQ], v_bd[:, IPT * t + b, j, :], start=True, stop=True)
                    last.then_inc(att_mm, 1)
                for t in range(NT):
                    pe.wait_ge(att_ready, NT * a + t + 1)
                    for c in range(2):
                        last = nc.tensor.transpose(ps[:, 2 * t + 1, c * P:(c + 1) * P], att[:, t, c * P:(c + 1) * P], ident)
                    last.then_inc(attT_mm, 1)
                for t in range(NT):
                    pe.wait_ge(attT_sb, NT * a + t + 1)
                    for c, rows in ((0, DA), (1, DB)):
                        last = nc.tensor.matmul(ps[:, 2 * t, 0:D], attT[0:rows, t, c, :], wo[a][0:rows, c, :], start=(c == 0), stop=(c == 1))
                    last.then_inc(proj_mm, 1)

            turn_tokens(0)
            pe.wait_ge(attn0_dma, 16 * ATTN0_LOADS)
            pe.wait_ge(xnT_sb, NT)
            for c in range(3):
                for k, rows in ((0, DA), (1, DB)):
                    last = nc.tensor.matmul(ps[:, c, :], wqkv0[0:rows, k, c * P:(c + 1) * P], xnT[0:rows, k, :], start=(k == 0), stop=(k == 1))
                last.then_inc(qkT0_mm, 1)
            values(wqkv0[:, :, 2 * D:3 * D])
            nc.tensor.transpose(ps[:, 3, 0:HD], omega8[:, :, :].rearrange("f h d -> f (h d)"), ident[0:HD, 0:HD]).then_inc(omega_mm, 1)
            pe.wait_ge(omega_sb, 1)
            pe.wait_ge(qkT0_sb, 3)
            for t in range(NT):
                for c in range(3):
                    last = nc.tensor.matmul(ps[:, t, c * P:(c + 1) * P], qkT0[:, c, t * P:(t + 1) * P], omega_bd[:, :], start=True, stop=True)
                last.then_inc(qk_mm, 1)
            attention(0)
            turn_tokens(1)
            pe.wait_ge(route_dma, 16 * ROUTE_LOADS)
            for t in range(NT):
                pe.wait_ge(xnT_sb, NT + t + 1)
                for k, rows in ((0, DA), (1, DB)):
                    last = nc.tensor.matmul(ps[:, 0, t * (G + NE):(t + 1) * (G + NE)], xnT[0:rows, k, t * P:(t + 1) * P], wroute[0:rows, k, :],
                                            start=(k == 0), stop=(k == 1))
            last.then_inc(logits_mm, 1)
            for c in range(KH):
                nc.tensor.transpose(ps[:, 5, c * NE:(c + 1) * NE], b1_rows[:, c * P:(c + 1) * P], ident[0:NE, 0:NE])
            pe.wait_ge(chosen_ready, 1)
            seen = ps[:, 2, 0:(NT + 1) * NE].rearrange("p (t e) -> p t e", e=NE)
            nc.tensor.matmul(seen[:, 0:NT], const("before"), chosen[:, :, :], start=True, stop=False)
            nc.tensor.matmul(seen[:, NT], const("ones"), chosen[:, NT - 1, :], start=False, stop=False)
            for later in range(1, NT + 1):
                n = min(NT + 1 - later, NT - 1)
                last = nc.tensor.matmul(seen[:, later:later + n], const("ones"), chosen[:, 0:n, :], start=False, stop=(later == NT))
            last.then_inc(counts_mm, 1)
            for t in range(NT):
                last = nc.tensor.matmul(ps[0:NE, 3, 0:1], chosen[:, t, :], const("ones", P, 1), start=(t == 0), stop=(t == NT - 1))
            last.then_inc(count_col_mm, 1)
            pe.wait_ge(extra_col_ready, 1)
            nc.tensor.matmul(ps[0:NE, 4, 0:1], const("before", NE, NE), extra_col[:, :], start=True, stop=True).then_inc(extra_at_mm, 1)
            pe.wait_ge(ov_onehot_ready, 1)
            for c in range(KH):
                nc.tensor.matmul(ps[:, 5, 256 + c * NOV:256 + (c + 1) * NOV], b1_rows[:, c * P:(c + 1) * P], ov_onehot[:, :], start=True, stop=True)
            nc.tensor.matmul(ps[0:1, 5, 384:384 + NOV], const("row", NE), ov_onehot[:, :], start=True, stop=True).then_inc(ov_mm, 1)
            pe.wait_ge(comb_ready, 1)
            for t in range(NT):
                last = nc.tensor.transpose(ps[0:NE, 1, t * P:(t + 1) * P], comb[:, t, :], ident)
            last.then_inc(combT_mm, 1)
            pe.wait_ge(combT_sb, 1)
            for t in range(NT):
                last = nc.tensor.matmul(ps[:, 6 + t // 2, (t % 2) * D:(t % 2 + 1) * D], combT[:, t * P:(t + 1) * P], b2_rows[:, :], start=True, stop=True)
            last.then_inc(b2_mm, 1)

            tiles = number_of_ov_tiles(pe)
            pe.wait_ge(b1T_sb, 2)
            pe.wait_ge(b2_added, 2)
            pe.wait_ge(ffn_dma, 16 * FFN_LOADS)
            for e in range(N1):
                if e >= 4:
                    pe.wait_ge(ffn_w13T_sb, 2 * (e - 3))
                    pe.wait_ge(ffn_w2T_sb, e - 3)
                bank = 2 * (e % 4)
                for m in range(2):
                    nc.tensor.transpose(ps[:, bank, m * P:(m + 1) * P], w13_raw[:, e, m, :], ident)
                nc.tensor.transpose(ps[:, bank, 2 * P:3 * P], w13_raw_tail[:, e, :], ident)
                nc.tensor.transpose(ps[:, bank + 1, 0:DA], w2_raw[:, e, :], ident)
                nc.tensor.transpose(ps[:, bank + 1, DA:D], w2_raw_tail[:, e, :], ident[0:DB, 0:DB]).then_inc(ffn_wT_mm, 1)
            pe.wait_ge(ffn_w13T_sb, 2 * (N1 - 3))
            for c in range(2):
                last = nc.tensor.transpose(ps[:, 2, c * E1:(c + 1) * E1], gate_rows[:, c * P:(c + 1) * P], ident[0:E1, 0:E1])
            last.then_inc(ffn_wT_mm, 1)
            pe.wait_ge(ffn_w13T_sb, 2 * N1 + 1)
            pe.wait_ge(ffn_w2T_sb, N1)

            def rows_in(i, u):
                pe.wait_ge(x_dma[u], 16 * (i + 1))
                for c in range(2):
                    last = nc.tensor.transpose(ps[:, u % 2, c * P:(c + 1) * P], x_rows[:, u, c * P:(c + 1) * P], ident)
                last.then_inc(rowsT_mm, 1)

            def up_in(i, u):
                buf = u % 2
                pe.wait_ge(w_dma[u], 16 * W_LOADS * (i + 1))
                pe.wait_ge(rowsT_sb, i * RING + u + 1)
                for c in range(KH // 2):
                    for half in range(2):
                        nc.tensor.matmul(ps[:, 2 + 2 * buf + half, c * P:(c + 1) * P], w1[:, u, (c + 3 * half) * P:(c + 3 * half + 1) * P],
                                         x_rowsT[:, buf, 0, :], start=True, stop=False)
                    for half in range(2):
                        rows = slice(half * DB, (half + 1) * DB)
                        last = nc.tensor.matmul(ps[:, 2 + 2 * buf + half, c * P:(c + 1) * P], w1_tail[rows, u, c * P:(c + 1) * P],
                                                x_rowsT[rows, buf, 1, :], start=False, stop=True)
                last.then_inc(up_mm, 1)

            def experts(i, ov_round, first):
                for u in range(RING):
                    with where_tile(pe, tiles, ov_round, u):
                        with where_tile(pe, tiles, ov_round, u + 1):
                            up_in(i + (u + 1) // RING, (u + 1) % RING)
                        with where_tile(pe, tiles, ov_round, u + 2):
                            rows_in(i + (u + 2) // RING, (u + 2) % RING)
                        pe.wait_ge(gelu_done, i * RING + u + 1)
                        if not (first and u < 2):
                            pe.wait_ge(y_ready, i * RING + u - 1)
                        for c in range(KH):
                            last = nc.tensor.matmul(ps[:, 6 + u % 2, 0:D], hidden[:, u % 2, c, :], w2[:, u, c, :], start=(c == 0), stop=(c == KH - 1))
                        last.then_inc(down_mm, 1)

            rows_in(0, 0)
            rows_in(0, 1)
            up_in(0, 0)
            rounds(pe, tiles, experts)
            pe.wait_ge(y_ready, tiles + NE)
            turn_tokens(2)
            pe.wait_ge(attn1_dma, 16 * ATTN1_LOADS)
            for t in range(NT):
                pe.wait_ge(xnT_sb, 2 * NT + (NT if t == 3 else t + 1))
                for k, rows in ((0, DA), (1, DB)):
                    last = nc.tensor.matmul(ps[:, t, 0:2 * D], xnT[0:rows, k, t * P:(t + 1) * P], wqkv1[0:rows, k, 0:2 * D], start=(k == 0), stop=(k == 1))
                last.then_inc(qk_mm, 1)
            values(wqkv1[:, :, 2 * D:3 * D])
            attention(1)
            turn_tokens(3)
            for t in range(NT):
                pe.wait_ge(xnT_sb, 3 * NT + t + 1)
                for k, rows in ((0, DA), (1, DB)):
                    last = nc.tensor.matmul(ps[:, 4, t * E1:(t + 1) * E1], xnT[0:rows, k, t * P:(t + 1) * P], gate_wT[0:rows, k, :], start=(k == 0), stop=(k == 1))
            last.then_inc(gate_mm, 1)

            def up1(n, u, first=False):
                if not first:
                    pe.wait_ge(gated_ready, n - 1)
                w, wt = w13T[:, n], w13T_tail[:, n]
                for m in range(2):
                    nc.tensor.matmul(ps[:, 2 * u + m, :], w[:, m, :], xnT[:, 0, :], start=True, stop=False)
                for m in range(2):
                    rows = slice(m * DB, (m + 1) * DB)
                    last = nc.tensor.matmul(ps[:, 2 * u + m, :], wt[rows, :], xnT[rows, 1, :], start=False, stop=True)
                last.then_inc(up1_mm, 1)

            def down1(n, u, first=False):
                pe.wait_ge(gated_ready, n + 1)
                if not first:
                    pe.wait_ge(summed, n - 1)
                w = w2T[:, n]
                for t in range(NT):
                    last = nc.tensor.matmul(ps[:, 6 - 2 * u + t // 2, (t % 2) * D:(t % 2 + 1) * D], gated[:, u, t * P:(t + 1) * P], w, start=True, stop=True)
                last.then_inc(down1_mm, 1)

            up1(0, 0, True)
            up1(1, 1, True)
            down1(0, 0, True)
            pe.wait_ge(score_ready, 1)
            up1(2, 0)
            down1(1, 1, True)
            for i in range(1, N1 // 2):
                up1(2 * i + 1, 1)
                down1(2 * i, 0)
                up1(2 * i + 2, 0)
                down1(2 * i + 1, 1)
            down1(N1 - 1, 0)

        @block.vector
        def _(dve):
            steps = [0]

            def step(ins):
                steps[0] += 1
                ins.then_inc(dve_step, 1)
                return steps[0]

            def after(n):
                dve.wait_ge(dve_step, n)

            def layer_norm(r):
                dve.wait_ge(deviation, r + 1)
                after(step(dve.reciprocal(rstd[:, :, 0], rstd[:, :, 0])))
                for t in range(NT):
                    dve.tensor_scalar(xn[:, t, 0:D], h[:, t], mv[:, t, 0:1], rstd[:, t], ALU.subtract, ALU.mult)
                    dve.tensor_scalar(xn[:, t, D:XW], h[:, t, DA:D], mv[:, t, 0:1], rstd[:, t], ALU.subtract, ALU.mult).then_inc(xn_ready, 1)

            def token_moments(r, t):
                dve.wait_ge(h_ready, r * NT + t + 1)
                after(step(dve.bn_stats(stats[:, t], h[:, t])))
                dve.bn_aggr(mv[:, t], stats[:, t]).then_inc(moments, 1)

            def values_out(a):
                for g in range(2):
                    dve.wait_ge(v_mm, 2 * a + g + 1)
                    for q in range(2):
                        rows = slice(q * SEQ, (q + 1) * SEQ)
                        dve.tensor_tensor(v_bd[rows, 4 * g:4 * g + 4, :, q * VW:q * VW + HD],
                                          ps[rows, 6 + g, 0:2 * D].rearrange("p (b j d) -> p b j d", b=4, d=HD),
                                          bv[a][rows, :].rearrange("p (j d) -> p j d", d=HD).unsqueeze(1).to_broadcast([SEQ, 4, NPAIR, HD]),
                                          ALU.add).then_inc(v_sb, 1)

            def attention(a):
                for t in range(NT):
                    dve.wait_ge(scores_mm, NT * a + t + 1)
                    src = ps[:, 4 * (t % 2):4 * (t % 2) + 4, 0:HB * SEQ].rearrange("p i (j k) -> p i j k", j=HB)
                    dst = probs[:, t].rearrange("p (j i) k -> p i j k", i=HG)
                    mask = const("future" if a else "causal").unsqueeze(1).unsqueeze(1).to_broadcast([P, HG, HB, SEQ])
                    dve.tensor_tensor(dst, src, mask, ALU.add if a else ALU.mult).then_inc(scores_read, 1)
                    if a == 1:
                        dve.wait_ge(scores_read, NT * a + t + 1)
                        after(step(dve.tensor_reduce(rowmax[:, t], probs[:, t], X, ALU.max)))
                        dve.tensor_tensor(probs[:, t], probs[:, t], rowmax[:, t].unsqueeze(2).to_broadcast([P, H, SEQ]), ALU.subtract).then_inc(centred, 1)
                for t in range(NT):
                    dve.wait_ge(att_mm, NT * a + t + 1)
                    o = ps[:, 2 * t, 0:H * VW].rearrange("p (h c) -> p h c", c=VW)
                    if a == 0:
                        after(step(dve.tensor_scalar(rden[:, t], o[:, :, HD], RFM_EPS * HD, None, ALU.add)))
                        after(step(dve.reciprocal(rden[:, t], rden[:, t])))
                    else:
                        after(step(dve.reciprocal(rden[:, t], o[:, :, HD])))
                    dve.tensor_tensor(att[:, t, 0:D].rearrange("p (h c) -> p h c", c=HD), o[:, :, 0:HD],
                                      rden[:, t].unsqueeze(2).to_broadcast([P, H, HD]), ALU.mult).then_inc(att_ready, 1)
                for t in range(NT):
                    dve.wait_ge(proj_mm, NT * a + t + 1)
                    dve.wait_ge(hb_ready, NT * a + t + 1)
                    dve.tensor_tensor(h[:, t], ps[:, 2 * t, 0:D], hb[:, t], ALU.add).then_inc(h_ready, 1)
                    token_moments(2 * a + 1, t)

            dve.wait_ge(x_in_dma[0], 32)
            regroup_channel(dve.tensor_copy, 0).then_inc(x_by_col_ready[0], 1)
            for c in range(KP // 2):
                dve.wait_ge(wtokT_mm, 2 * c + 2)
                dve.tensor_copy(wtokT[:, 2 * c:2 * c + 2, :].rearrange("p k e -> p (k e)"), ps[:, c, 0:2 * D]).then_inc(wtokT_sb, 1)
            dve.wait_ge(x_in_dma[2], 32)
            regroup_channel(dve.tensor_copy, 2).then_inc(x_by_col_ready[2], 1)
            for n in range(1, 2 * NCH, 2):
                dve.wait_ge(patches_mm, n + 1)
                patch_job(dve.tensor_copy, n).then_inc(patches_dve, 1)
            dve.wait_ge(attn0_dma, 16 * ATTN0_LOADS)
            for t in range(NT):
                dve.wait_ge(embed_mm, t + 1)
                dve.tensor_tensor(h[:, t], ps[:, t % 3, 0:D], btok[:, :], ALU.add).then_inc(h_ready, 1)
                token_moments(0, t)
            layer_norm(0)
            dve.wait_ge(pads_zeroed, 5)
            values_out(0)
            dve.wait_ge(omega_mm, 1)
            dve.tensor_tensor(omega_bd[:, :].rearrange("p (h f) -> p h f", f=HD),
                              ps[:, 3, 0:HD].unsqueeze(1).to_broadcast([P, P // HD, HD]),
                              const("headblock").unsqueeze(2).to_broadcast([P, P // HD, HD]), ALU.mult).then_inc(omega_sb, 1)
            for t in range(NT):
                dve.wait_ge(qk_mm, t + 1)
                s = ps[:, t, 0:2 * D].rearrange("p (h f) -> p h f", f=HD)
                step(dve.tensor_reduce(fsum[:, t], s, X, ALU.add))
                step(dve.tensor_reduce(foff[:, t, 0:H], s[:, 0:H], X, ALU.max))
                after(step(dve.tensor_reduce(fmax[:, t], ps[:, t, D:2 * D], X, ALU.max)))
                step(dve.scalar_tensor_tensor(out=foff[:, t, 0:H], in0=fsum[:, t, 0:H], scalar=0.5, in1=foff[:, t, 0:H], op0=ALU.mult, op1=ALU.add))
                after(step(dve.tensor_scalar(foff[:, t, H:2 * H], fsum[:, t, H:2 * H], 0.5, fmax[:, t], ALU.mult, ALU.add)))
                dve.tensor_tensor(turned[:, t].rearrange("p (h f) -> p h f", f=HD), s,
                                  foff[:, t].unsqueeze(2).to_broadcast([P, 2 * H, HD]), ALU.subtract).then_inc(feat_centred, 1)
            attention(0)
            layer_norm(1)
            dve.wait_ge(route_dma, 16 * ROUTE_LOADS)
            dve.wait_ge(logits_mm, 1)
            lg = ps[:, 0, 0:NT * (G + NE)].rearrange("p (t c) -> p t c", t=NT)
            step(dve.tensor_tensor(ggl[:, :, :], lg[:, :, 0:G], broute[:, 0:G].unsqueeze(1).to_broadcast([P, NT, G]), ALU.add))
            after(step(dve.tensor_tensor(gel[:, :, :].rearrange("p (t g) e -> p t (g e)", t=NT), lg[:, :, G:G + NE],
                                         broute[:, G:G + NE].unsqueeze(1).to_broadcast([P, NT, NE]), ALU.add)))

            def top2(jobs):
                def each(ins):
                    after([step(ins(*job)) for job in jobs][-1])

                for r in range(2):
                    src = (lambda v, rest: rest) if r else (lambda v, rest: v)
                    each(lambda v, hot, work, rest, best, at, n: dve.tensor_reduce(best[r], src(v, rest), X, ALU.max))
                    each(lambda v, hot, work, rest, best, at, n: dve.tensor_tensor(
                        work, src(v, rest), best[r].unsqueeze(2).to_broadcast(list(work.shape)), ALU.is_equal))
                    each(lambda v, hot, work, rest, best, at, n: dve.tensor_tensor(
                        work, work, const("earlier")[:, EG - n:EG].unsqueeze(1).to_broadcast(list(work.shape)), ALU.mult))
                    each(lambda v, hot, work, rest, best, at, n: dve.tensor_reduce(at, work, X, ALU.max))
                    each(lambda v, hot, work, rest, best, at, n: dve.tensor_tensor(
                        hot[r], work, at.unsqueeze(2).to_broadcast(list(work.shape)), ALU.is_equal))
                    if r == 0:
                        each(lambda v, hot, work, rest, best, at, n: dve.scalar_tensor_tensor(
                            out=rest, in0=hot[0], scalar=-BIG, in1=v, op0=ALU.mult, op1=ALU.add))

            def group_job(values):
                return (values, [pick_g[:, r] for r in range(2)], work_g[:, :, :], rest_g[:, :, :],
                        [best[:, r, 0:NT] for r in range(2)], first_of[:, 0:NT], G)

            by_group = "p t (g e) -> p (t g) e"
            hot_e = [pick_e[:, r].rearrange(by_group, g=G) for r in range(2)]
            top2([group_job(ggl[:, :, :]),
                  (gel[:, :, :], hot_e, work_e[:, :, :], rest_e[:, :, :], [best[:, r, NT:] for r in range(2)], first_of[:, NT:], EG)])
            step(dve.tensor_tensor(sel_g[:, :, :], pick_g[:, 0], pick_g[:, 1], ALU.add))
            after(step(dve.tensor_tensor(sel_e[:, :, :], hot_e[0], hot_e[1], ALU.add)))

            def by_expert(x):
                return x.rearrange("p t g -> p (t g)").unsqueeze(2).to_broadcast([P, NT * G, EG])

            dve.tensor_tensor(chosen[:, :, :].rearrange(by_group, g=G), sel_e[:, :, :], by_expert(sel_g[:, :, :]), ALU.mult).then_inc(chosen_ready, 1)
            dve.tensor_tensor(gates[:, 1, :], best[:, 1, :], best[:, 0, :], ALU.subtract).then_inc(gates_centred, 1)
            for k in range(PICKS):
                step(dve.tensor_tensor(pick[:, k].rearrange(by_group, g=G), hot_e[k % 2], by_expert(pick_g[:, k // 2]), ALU.mult))
            after(step(dve.memset(extra[:, 0:1], 0.0)))
            dve.wait_ge(counts_mm, 1)
            count, place = ps[:, 2, NT * NE:(NT + 1) * NE], ps[:, 2, 0:NT * NE].rearrange("p (t e) -> p t e", t=NT)

            def extra_tiles(dst, src):
                after(step(dve.tensor_scalar(dst, src, float(P), None, ALU.is_gt)))
                for m in range(2, NT):
                    ins = dve.scalar_tensor_tensor(out=dst, in0=src, scalar=float(m * P), in1=dst, op0=ALU.is_gt, op1=ALU.add)
                    if m < NT - 1:
                        after(step(ins))
                return ins

            step(dve.tensor_tensor(home[:, :, :], place, const("first_slot").unsqueeze(1).to_broadcast([P, NT, NE]), ALU.add))
            after(step(extra_tiles(extra[:, 1:1 + NE], count)))
            after(step(dve.tensor_tensor_scan(extra_sum[:, :], const("ones", P, 1 + NE), extra[:, :], 0.0, ALU.mult, ALU.add)))
            after(step(dve.scalar_tensor_tensor(out=shift[:, :], in0=extra_sum[:, 0:NE], scalar=float(P), in1=const("ov_shift"), op0=ALU.mult, op1=ALU.add)))
            after(step(dve.scalar_tensor_tensor(out=slot[:, :, :], in0=place, scalar=float(P) - 0.5, in1=shift[:, :].unsqueeze(1).to_broadcast([P, NT, NE]),
                                                op0=ALU.is_gt, op1=ALU.mult)))
            after(step(dve.tensor_tensor(slot[:, :, :], home[:, :, :], slot[:, :, :], ALU.add)))

            def take(dst, values):
                after(step(dve.tensor_tensor(picked[:, :, :].rearrange("p (k t) e -> p k (t e)", k=PICKS),
                                             pick[:, :, :, :].rearrange("p k t e -> p k (t e)"),
                                             values.rearrange("p t e -> p (t e)").unsqueeze(1).to_broadcast([P, PICKS, NT * NE]), ALU.mult)))
                return dve.tensor_reduce(dst, picked[:, :, :], X, ALU.add)

            after(step(take(pick_slot[:, :], slot[:, :, :])))
            dve.tensor_copy(pick_slot_u[:, :], pick_slot[:, :]).then_inc(slots_ready, 1)
            dve.tensor_copy(ov_tiles[0:1, 0:1], extra_sum[0:1, NE:NE + 1]).then_inc(tile_info_ready, 1)
            dve.wait_ge(count_col_mm, 1)
            extra_tiles(extra_col[:, :], ps[0:NE, 3, 0:1]).then_inc(extra_col_ready, 1)
            dve.wait_ge(extra_at_mm, 1)
            after(step(dve.tensor_copy(extra_at[:, :], ps[0:NE, 4, 0:1])))
            step(dve.tensor_tensor(extra_end[:, :], extra_at[:, :], extra_col[:, :], ALU.add))
            after(step(dve.tensor_scalar(ov_from[:, :], const("index", NE), extra_at[:, 0:1], None, ALU.is_ge)))
            dve.scalar_tensor_tensor(out=ov_onehot[:, :], in0=const("index", NE), scalar=extra_end[:, 0:1], in1=ov_from[:, :],
                                     op0=ALU.is_lt, op1=ALU.mult).then_inc(ov_onehot_ready, 1)
            dve.wait_ge(gates_exp, 1)
            after(step(dve.tensor_scalar(gate_sum[:, :], gates[:, 1, :], 1.0, None, ALU.add)))
            after(step(dve.reciprocal(gates[:, 0, :], gate_sum[:, :])))
            after(step(dve.tensor_tensor(gates[:, 1, :], gates[:, 1, :], gates[:, 0, :], ALU.mult)))
            for r in range(2):
                step(dve.tensor_tensor(group_gate[:, r], pick_g[:, r], gates[:, r, 0:NT].unsqueeze(2).to_broadcast([P, NT, G]), ALU.mult))
            work = [work_e[:, :, :], rest_e[:, :, :]]
            for r in range(2):
                n = step(dve.tensor_tensor(work[r], hot_e[r], gates[:, r, NT:].unsqueeze(2).to_broadcast([P, NT * G, EG]), ALU.mult))
            after(n)
            step(dve.tensor_tensor(group_gate[:, 0], group_gate[:, 0], group_gate[:, 1], ALU.add))
            after(step(dve.tensor_tensor(work[0], work[0], work[1], ALU.add)))
            dve.tensor_tensor(comb[:, :, :].rearrange(by_group, g=G), work[0], by_expert(group_gate[:, 0]), ALU.mult).then_inc(comb_ready, 1)
            dve.wait_ge(comb_ready, 1)
            step(take(pick_w[:, :], comb[:, :, :]))
            dve.wait_ge(b2_mm, 1)
            for g in range(2):
                dve.tensor_tensor(hb[:, 2 * g:2 * g + 2, :], ps[:, 6 + g, 0:2 * D].rearrange("p (t d) -> p t d", t=2),
                                  h[:, 2 * g:2 * g + 2, :], ALU.add).then_inc(b2_added, 1)

            for e in range(N1):
                dve.wait_ge(ffn_wT_mm, e + 1)
                dve.tensor_copy(w2T[:, e], ps[:, 2 * (e % 4) + 1, 0:D]).then_inc(ffn_w2T_sb, 1)
            tiles = number_of_ov_tiles(dve)

            def rows_out(i, u):
                dve.wait_ge(rowsT_mm, i * RING + u + 1)
                dve.tensor_copy(x_rowsT[:, u % 2], ps[:, u % 2, 0:2 * P].rearrange("p (c n) -> p c n", c=2)).then_inc(rowsT_sb, 1)

            def results(i, ov_round, first):
                for u in range(RING):
                    with where_tile(dve, tiles, ov_round, u):
                        with where_tile(dve, tiles, ov_round, u + 2):
                            rows_out(i + (u + 2) // RING, (u + 2) % RING)
                        dve.wait_ge(down_mm, i * RING + u + 1)
                        if not first:
                            dve.wait_ge(y_dma[u], 16 * i)
                        dve.tensor_copy(y_rows[:, u, :], ps[:, 6 + u % 2, 0:D]).then_inc(y_ready, 1)

            rows_out(0, 0)
            rows_out(0, 1)
            rounds(dve, tiles, results)
            after(steps[0])
            for pair in range(0, NT, 2):
                dve.wait_ge(y_back_dma[pair], 16)
                dve.wait_ge(y_back_dma[pair + 1], 16)
                for k in range(PICKS):
                    for t in (pair, pair + 1):
                        ins = dve.scalar_tensor_tensor(out=(h if k == PICKS - 1 else hb)[:, t], in0=y_back[:, t, k],
                                                       scalar=pick_w[:, k * NT + t:k * NT + t + 1], in1=hb[:, t], op0=ALU.mult, op1=ALU.add)
                        if k == PICKS - 1:
                            ins.then_inc(h_ready, 1)
                        else:
                            n = step(ins)
                    if k < PICKS - 1:
                        after(n)
                for t in (pair, pair + 1):
                    token_moments(2, t)
            layer_norm(2)
            def rotate(t):
                x2 = turned[:, t].rearrange("p (m n r) -> p m n r", m=2, r=2)
                s2 = rope_swap[:, t, 0:2 * D].rearrange("p (m n r) -> p m n r", m=2, r=2)
                sin = const("rope_sin").rearrange("p (n r) -> p n r", r=2)
                dve.wait_ge(qk_biased, t + 1)
                for r in range(2):
                    n = step(dve.tensor_tensor(s2[:, :, :, r], x2[:, :, :, 1 - r], sin[:, :, r].unsqueeze(1).to_broadcast([P, 2, D // 2]), ALU.mult))
                after(n)
                dve.wait_ge(rope_cos_part, t + 1)
                dve.tensor_tensor(qk_pad[:, t, :, 0:HD], fexp[:, t], rope_swap[:, t, 0:2 * D].rearrange("p (h f) -> p h f", f=HD), ALU.add).then_inc(qk_pad_ready, 1)

            for t in range(NT):
                dve.wait_ge(qk_mm, NT + t + 1)
                dve.tensor_tensor(turned[:, t], ps[:, t, 0:2 * D], bqk1[:, :], ALU.add).then_inc(qk_biased, 1)
                if t >= 1:
                    rotate(t - 1)
            rotate(NT - 1)
            values_out(1)
            attention(1)
            layer_norm(3)

            dve.wait_ge(score_ready, 1)
            dve.wait_ge(ffn_dma, 16 * FFN_LOADS)
            after(step(dve.tensor_tensor(biased[:, :, :], score[:, :, :], gate_b[:, :].unsqueeze(1).to_broadcast([P, NT, E1]), ALU.add)))
            after(step(dve.tensor_reduce(group_sum[:, :, :], biased[:, :, :].rearrange("p t (g e) -> p t g e", g=G), X, ALU.add)))
            top2([group_job(group_sum[:, :, :])])
            after(step(dve.tensor_tensor(sel_g[:, :, :], pick_g[:, 0], pick_g[:, 1], ALU.add)))
            after(step(dve.tensor_scalar(shut[:, :, :], sel_g[:, :, :], 1.0, BIG, ALU.subtract, ALU.mult)))
            b3 = biased[:, :, :].rearrange("p t (g e) -> p (t g) e", g=G)
            after(step(dve.tensor_tensor(b3, b3, shut[:, :, :].rearrange("p t g -> p (t g)").unsqueeze(2).to_broadcast([P, NT * G, E1 // G]), ALU.add)))
            top2([(biased[:, :, :], chosen_1, work_e[:, 0:NT, :], rest_e[:, 0:NT, :], [best[:, r, 0:NT] for r in range(2)], first_of[:, 0:NT], E1)])
            after(step(dve.tensor_tensor(cw[:, :, :], chosen_1[0], chosen_1[1], ALU.add)))
            after(step(dve.tensor_tensor(cw[:, :, :], cw[:, :, :], score[:, :, :], ALU.mult)))
            after(step(dve.tensor_reduce(score_sum[:, :], cw[:, :, :], X, ALU.add)))
            after(step(dve.tensor_scalar(score_sum[:, :], score_sum[:, :], 1e-6, None, ALU.add)))
            after(step(dve.reciprocal(score_sum[:, :], score_sum[:, :])))
            after(step(dve.tensor_tensor(cw[:, :, :], cw[:, :, :], score_sum[:, :].unsqueeze(2).to_broadcast([P, NT, E1]), ALU.mult)))

            def gate_product(n, u, first=False):
                dve.wait_ge(silu_done, n + 1)
                if not first:
                    dve.wait_ge(down1_mm, n - 1)
                dve.tensor_tensor(gated[:, u, :], silu[:, u, :], ps[:, 2 * u + 1, :], ALU.mult).then_inc(gated_ready, 1)

            def add_expert(n, u):
                dve.wait_ge(down1_mm, n + 1)
                dve.wait_ge(summed, n)
                for t in range(NT):
                    ins = dve.scalar_tensor_tensor(out=h[:, t], in0=ps[:, 6 - 2 * u + t // 2, (t % 2) * D:(t % 2 + 1) * D],
                                                   scalar=cw[:, t, bass.ds(n - 1, 1)], in1=h[:, t], op0=ALU.mult, op1=ALU.add)
                ins.then_inc(summed, 1)

            gate_product(0, 0, True)
            gate_product(1, 1, True)
            dve.wait_ge(down1_mm, 1)
            dve.wait_ge(h_ready, LAST_H * NT)
            for g in range(2):
                hg = h[:, 2 * g:2 * g + 2, :]
                ins = dve.tensor_tensor(hg, ps[:, 6 + g, 0:2 * D].rearrange("p (t d) -> p t d", t=2), hg, ALU.add)
            ins.then_inc(summed, 1)
            gate_product(2, 0)
            add_expert(1, 1)
            with dve.Fori(1, N1 // 2) as i:
                gate_product(2 * i + 1, 1)
                add_expert(2 * i, 0)
                gate_product(2 * i + 2, 0)
                add_expert(2 * i + 1, 1)
            add_expert(N1 - 1, 0)


TILE_INFO = 2
W_LOADS = 4
ROUTE_LOADS = 4 + 4
TURN_BANK = ((4, 6, 4, 6), (4, 0, 2, 4))
PATCH_BANK = [3, 4, 5, 6, 7, 3]
ATTN0_LOADS = 1 + 2 + 1 + 2 + 1 + 2 + 1
ATTN1_LOADS = 6 + 2 + 2 + 2 + 1
LAST_H = 4
FFN_LOADS = 8 + 4 + 3

_INS = ['x', 'L0_tok_W', 'L0_tok_b', 'L0_attn_w_inp', 'L0_attn_b_inp', 'L0_attn_w_out', 'L0_attn_b_out', 'L0_attn_omega',
        'L0_ffn_Wg', 'L0_ffn_bg', 'L0_ffn_Wge', 'L0_ffn_bge', 'L0_ffn_W1', 'L0_ffn_b1', 'L0_ffn_W2', 'L0_ffn_b2',
        'L1_attn_Wq', 'L1_attn_bq', 'L1_attn_Wk', 'L1_attn_bk', 'L1_attn_Wv', 'L1_attn_bv', 'L1_attn_Wo', 'L1_attn_bo',
        'L1_ffn_gate_weight', 'L1_ffn_gate_bias', 'L1_ffn_w1', 'L1_ffn_w2', 'L1_ffn_w3', 'L1_ffn_sw1', 'L1_ffn_sw2', 'L1_ffn_sw3']


def kernel(**inputs):
    import concourse.bacc as bacc
    from concourse.bass_utils import run_bass_kernel_spmd

    nc = bacc.Bacc("TRN2", target_bir_lowering=False, num_devices=1)
    arrays, dram = {}, {}
    for name in _INS:
        a = np.ascontiguousarray(inputs[name])
        arrays[f"in_{name}"] = a
        dram[name] = nc.dram_tensor(f"in_{name}", a.shape, F32, kind="ExternalInput").ap()
    arrays["shape_constants"] = shape_constants()
    consts = nc.dram_tensor("shape_constants", (P, NCONST), F32, kind="ExternalInput").ap()
    out = nc.dram_tensor("out", (NIMG, SEQ, D), F32, kind="ExternalOutput").ap()
    vit_tower(nc, dram, consts, out)
    return run_bass_kernel_spmd(nc, [arrays], core_ids=[0]).results[0]["out"]
```
